# Optimizing a Trainium2 kernel written in Bass

```python
import numpy as np
import jax
import jax.numpy as jnp

def _softmax(x, axis=-1):
    return jax.nn.softmax(x, axis=axis)

def _gelu(x):
    return jax.nn.gelu(x, approximate=True)

def _silu(x):
    return jax.nn.silu(x)

def _sigmoid(x):
    return jax.nn.sigmoid(x)

def _layernorm(x, axis=-1, eps=1e-05):
    m = jnp.mean(x, axis=axis, keepdims=True)
    v = jnp.var(x, axis=axis, keepdims=True)
    return (x - m) / jnp.sqrt(v + eps)

def _scatter_add(tgt, idx, src, axis=0):
    return tgt.at[idx].add(src)

def _segment_sum(src, seg, n):
    return jax.ops.segment_sum(src, seg, n)
kernel_name = 'mk_prb_d2_jaxref_r8_e9495f'

def setup_inputs(seed: int=0):
    np.random.seed(seed)
    _w = jnp.asarray

    def _L0_attn_setup():
        import jax, jax.numpy as jnp
        import numpy as np
        D = 128
        H = 16
        HD = D // H
        EPS = 1e-06

        def _rmsnorm(x, w):
            xf = x.astype(jnp.float32)
            var = jnp.mean(xf * xf, axis=-1, keepdims=True)
            return (w * (xf * jax.lax.rsqrt(var + EPS))).astype(x.dtype)
        key = jax.random.key(seed)
        ks = jax.random.split(key, 10)
        B, N = (2, 256)
        s = 0.02
        return {'x': jax.random.normal(ks[0], (B, N, D), jnp.float32), 'Wq': jax.random.normal(ks[1], (D, D + H), jnp.float32) * s, 'bq': jnp.zeros((D + H,), jnp.float32), 'Wk': jax.random.normal(ks[2], (D, D), jnp.float32) * s, 'bk': jnp.zeros((D,), jnp.float32), 'Wv': jax.random.normal(ks[3], (D, D), jnp.float32) * s, 'bv': jnp.zeros((D,), jnp.float32), 'Wo': jax.random.normal(ks[4], (D, D), jnp.float32) * s, 'bo': jnp.zeros((D,), jnp.float32), 'qn_w': jnp.ones((HD,), jnp.float32), 'kn_w': jnp.ones((HD,), jnp.float32)}
    _L0_attn_in = _L0_attn_setup()

    def _L0_ffn_setup():
        import jax, jax.numpy as jnp
        import numpy as np
        B, S, D = (2, 256, 128)
        E, K, F = (16, 2, 64)
        FS = 128
        key = jax.random.key(seed)
        ks = jax.random.split(key, 8)

        def w(k, shape, fan_in):
            return jax.random.normal(k, shape, jnp.float32) / np.sqrt(fan_in).astype(np.float32)
        return {'x': jax.random.normal(ks[0], (B, S, D), jnp.float32), 'Wr': w(ks[1], (D, E), D), 'Wg': w(ks[2], (E, D, F), D), 'Wu': w(ks[3], (E, D, F), D), 'Wd': w(ks[4], (E, F, D), F), 'Sg': w(ks[5], (D, FS), D), 'Su': w(ks[6], (D, FS), D), 'Sd': w(ks[7], (FS, D), FS)}
    _L0_ffn_in = _L0_ffn_setup()

    def _L1_attn_setup():
        import jax, jax.numpy as jnp
        import numpy as np
        NUM_HEADS = 16
        key = jax.random.key(seed)
        kx, kq, kk, kv = jax.random.split(key, 4)
        N, S, D = (2, 512, 128)
        scale = 1.0 / np.sqrt(D)
        x = jax.random.normal(kx, (N, S, D), dtype=jnp.float32)
        Wq = jax.random.normal(kq, (D, D), dtype=jnp.float32) * scale
        Wk = jax.random.normal(kk, (D, D), dtype=jnp.float32) * scale
        Wv = jax.random.normal(kv, (D, D), dtype=jnp.float32) * scale
        return {'x': x, 'Wq': Wq, 'Wk': Wk, 'Wv': Wv}
    _L1_attn_in = _L1_attn_setup()

    def _L1_ffn_setup():
        import jax, jax.numpy as jnp
        import numpy as np
        E = 8
        TOPK = 2

        def _moe_forward(x, Wg, W1, W2, W3):
            B, S, D = x.shape
            xt = x.reshape(-1, D)
            T = xt.shape[0]
            logits = xt @ Wg.T
            scores = jax.nn.softmax(logits, axis=-1)
            w, idx = jax.lax.top_k(scores, TOPK)
            w = w / (w.sum(axis=-1, keepdims=True) + 1e-20)
            cw = jnp.zeros((T, E), xt.dtype).at[jnp.arange(T)[:, None], idx].add(w)
            h = jax.nn.silu(jnp.einsum('td,ehd->teh', xt, W1)) * jnp.einsum('td,ehd->teh', xt, W3)
            out = jnp.einsum('teh,edh->ted', h, W2)
            y = jnp.einsum('te,ted->td', cw, out)
            return y.reshape(B, S, D)
        key = jax.random.key(seed)
        k0, k1, k2, k3, k4 = jax.random.split(key, 5)
        B, S, D, H = (1, 256, 128, 352)
        scale = 0.02
        x = jax.random.normal(k0, (B, S, D), jnp.float32)
        Wg = jax.random.normal(k1, (E, D), jnp.float32) * scale
        W1 = jax.random.normal(k2, (E, H, D), jnp.float32) * scale
        W2 = jax.random.normal(k3, (E, D, H), jnp.float32) * scale
        W3 = jax.random.normal(k4, (E, H, D), jnp.float32) * scale
        return {'x': x, 'Wg': Wg, 'W1': W1, 'W2': W2, 'W3': W3}
    _L1_ffn_in = _L1_ffn_setup()
    _d = {'L0_attn_x': _L0_attn_in['x'], 'L0_attn_Wq': _L0_attn_in['Wq'], 'L0_attn_bq': _L0_attn_in['bq'], 'L0_attn_Wk': _L0_attn_in['Wk'], 'L0_attn_bk': _L0_attn_in['bk'], 'L0_attn_Wv': _L0_attn_in['Wv'], 'L0_attn_bv': _L0_attn_in['bv'], 'L0_attn_Wo': _L0_attn_in['Wo'], 'L0_attn_bo': _L0_attn_in['bo'], 'L0_attn_qn_w': _L0_attn_in['qn_w'], 'L0_attn_kn_w': _L0_attn_in['kn_w'], 'L0_ffn_Wr': _L0_ffn_in['Wr'], 'L0_ffn_Wg': _L0_ffn_in['Wg'], 'L0_ffn_Wu': _L0_ffn_in['Wu'], 'L0_ffn_Wd': _L0_ffn_in['Wd'], 'L0_ffn_Sg': _L0_ffn_in['Sg'], 'L0_ffn_Su': _L0_ffn_in['Su'], 'L0_ffn_Sd': _L0_ffn_in['Sd'], 'L1_attn_Wq': _L1_attn_in['Wq'], 'L1_attn_Wk': _L1_attn_in['Wk'], 'L1_attn_Wv': _L1_attn_in['Wv'], 'L1_ffn_Wg': _L1_ffn_in['Wg'], 'L1_ffn_W1': _L1_ffn_in['W1'], 'L1_ffn_W2': _L1_ffn_in['W2'], 'L1_ffn_W3': _L1_ffn_in['W3']}
    _x0 = _d['L0_attn_x']
    _d['L0_attn_x'] = jax.random.normal(jax.random.fold_in(jax.random.key(seed), 1), (4, 512, 128), dtype=_x0.dtype)
    del _x0
    return _d

def reference(L0_attn_x, L0_attn_Wq, L0_attn_bq, L0_attn_Wk, L0_attn_bk, L0_attn_Wv, L0_attn_bv, L0_attn_Wo, L0_attn_bo, L0_attn_qn_w, L0_attn_kn_w, L0_ffn_Wr, L0_ffn_Wg, L0_ffn_Wu, L0_ffn_Wd, L0_ffn_Sg, L0_ffn_Su, L0_ffn_Sd, L1_attn_Wq, L1_attn_Wk, L1_attn_Wv, L1_ffn_Wg, L1_ffn_W1, L1_ffn_W2, L1_ffn_W3):

    def _L0_attn_ref(x, Wq, bq, Wk, bk, Wv, bv, Wo, bo, qn_w, kn_w):
        import jax, jax.numpy as jnp
        import numpy as np
        D = 128
        H = 16
        HD = D // H
        EPS = 1e-06

        def _rmsnorm(x, w):
            xf = x.astype(jnp.float32)
            var = jnp.mean(xf * xf, axis=-1, keepdims=True)
            return (w * (xf * jax.lax.rsqrt(var + EPS))).astype(x.dtype)
        B, N, _ = x.shape
        qg = x @ Wq + bq
        Q, gate = (qg[..., :D], qg[..., D:])
        K = x @ Wk + bk
        V = x @ Wv + bv
        Q = Q.reshape(B, N, H, HD).transpose(0, 2, 1, 3)
        K = K.reshape(B, N, H, HD).transpose(0, 2, 1, 3)
        V = V.reshape(B, N, H, HD).transpose(0, 2, 1, 3)
        Q = _rmsnorm(Q, qn_w)
        K = _rmsnorm(K, kn_w)
        scores = jnp.einsum('bhqd,bhkd->bhqk', Q, K) / jnp.sqrt(jnp.float32(HD))
        attn = jax.nn.softmax(scores.astype(jnp.float32), axis=-1).astype(Q.dtype)
        out = jnp.einsum('bhqk,bhkd->bhqd', attn, V)
        out = out.transpose(0, 2, 1, 3)
        out = out * jax.nn.sigmoid(gate)[..., None]
        out = out.reshape(B, N, D)
        return out @ Wo + bo

    def _L0_ffn_ref(x, Wr, Wg, Wu, Wd, Sg, Su, Sd):
        import jax, jax.numpy as jnp
        import numpy as np
        B, S, D = (2, 256, 128)
        E, K, F = (16, 2, 64)
        FS = 128
        b, s, d = x.shape
        T = b * s
        xf = x.reshape(T, d)
        shared = jax.nn.silu(xf @ Sg) * (xf @ Su) @ Sd
        probs = jax.nn.softmax(xf @ Wr, axis=-1)
        topk_p, topk_i = jax.lax.top_k(probs, K)
        n_exp = Wr.shape[1]
        cw = jnp.zeros((T, n_exp), x.dtype).at[jnp.arange(T)[:, None], topk_i].add(topk_p)

        def step(acc, ew):
            wg, wu, wd, c = ew
            y = jax.nn.silu(xf @ wg) * (xf @ wu) @ wd
            return (acc + y * c[:, None], None)
        routed, _ = jax.lax.scan(step, jnp.zeros_like(xf), (Wg, Wu, Wd, cw.T))
        return (routed + shared).reshape(b, s, d)

    def _L1_attn_ref(x, Wq, Wk, Wv):
        import jax, jax.numpy as jnp
        import numpy as np
        NUM_HEADS = 16
        N, S, D = x.shape
        H = NUM_HEADS
        hd = D // H
        q = (x @ Wq.T).reshape(N, S, H, hd).transpose(0, 2, 1, 3)
        k = (x @ Wk.T).reshape(N, S, H, hd).transpose(0, 2, 1, 3)
        v = (x @ Wv.T).reshape(N, S, H, hd).transpose(0, 2, 1, 3)
        energy = jnp.einsum('nhqd,nhkd->nhqk', q, k)
        attn = jax.nn.softmax(energy / jnp.sqrt(jnp.float32(hd)), axis=3)
        out = jnp.einsum('nhql,nhld->nhqd', attn, v)
        return out.transpose(0, 2, 1, 3).reshape(N, S, D)

    def _L1_ffn_ref(x, Wg, W1, W2, W3):
        import jax, jax.numpy as jnp
        import numpy as np
        E = 8
        TOPK = 2

        def _moe_forward(x, Wg, W1, W2, W3):
            B, S, D = x.shape
            xt = x.reshape(-1, D)
            T = xt.shape[0]
            logits = xt @ Wg.T
            scores = jax.nn.softmax(logits, axis=-1)
            w, idx = jax.lax.top_k(scores, TOPK)
            w = w / (w.sum(axis=-1, keepdims=True) + 1e-20)
            cw = jnp.zeros((T, E), xt.dtype).at[jnp.arange(T)[:, None], idx].add(w)
            h = jax.nn.silu(jnp.einsum('td,ehd->teh', xt, W1)) * jnp.einsum('td,ehd->teh', xt, W3)
            out = jnp.einsum('teh,edh->ted', h, W2)
            y = jnp.einsum('te,ted->td', cw, out)
            return y.reshape(B, S, D)
        return _moe_forward(x, Wg, W1, W2, W3)
    x = L0_attn_x
    xn = _layernorm(x, axis=-1)
    x = x + _L0_attn_ref(xn, L0_attn_Wq, L0_attn_bq, L0_attn_Wk, L0_attn_bk, L0_attn_Wv, L0_attn_bv, L0_attn_Wo, L0_attn_bo, L0_attn_qn_w, L0_attn_kn_w) + _L0_ffn_ref(xn, L0_ffn_Wr, L0_ffn_Wg, L0_ffn_Wu, L0_ffn_Wd, L0_ffn_Sg, L0_ffn_Su, L0_ffn_Sd)
    xn = _layernorm(x, axis=-1)
    x = x + _L1_attn_ref(xn, L1_attn_Wq, L1_attn_Wk, L1_attn_Wv) + _L1_ffn_ref(xn, L1_ffn_Wg, L1_ffn_W1, L1_ffn_W2, L1_ffn_W3)
    return x

_drawn_inputs = setup_inputs


def setup_inputs(seed=0):
    import zlib

    import numpy as np

    out = dict(_drawn_inputs(seed))
    spreads = {'L0_attn_bq': (0.0, 0.8),
     'L0_attn_bk': (0.0, 0.8),
     'L0_attn_bv': (0.0, 0.653),
     'L0_attn_bo': (0.0, 0.1),
     'L0_attn_qn_w': (1.0, 0.6),
     'L0_attn_kn_w': (1.0, 0.6)}
    factors = {'L0_attn_Wq': 8.0,
     'L0_attn_Wk': 8.0,
     'L0_attn_Wv': 8.0,
     'L0_attn_Wo': 5.08,
     'L1_ffn_Wg': 8.0,
     'L1_ffn_W1': 8.0,
     'L1_ffn_W2': 8.0,
     'L1_ffn_W3': 8.0,
     'L1_attn_Wq': 2.84,
     'L1_attn_Wk': 2.796}
    for name, (base, spread) in spreads.items():
        noise = np.random.default_rng([zlib.crc32(name.encode()), seed]).standard_normal(out[name].shape)
        drawn = base * np.exp(spread * noise) if base else spread * noise
        out[name] = jnp.asarray(drawn.astype(out[name].dtype))
    for name, factor in factors.items():
        out[name] = (out[name] * factor).astype(out[name].dtype)
    return out
```

```python
import concourse.bass as bass
from concourse import mybir
from contextlib import ExitStack

F32 = mybir.dt.float32
BF16 = mybir.dt.bfloat16
ACT = mybir.ActivationFunctionType
ALU = mybir.AluOpType
AXIS = mybir.AxisListType

B, N, D = 4, 512, 128
H, HD = 16, 8
P = 128
J = N // P
G, HG = 4, 4
VW = 32
STACK = 6 * HD
MAXROWS = 3
SLOTS = 3
BANK = 512
R = 3
LN_EPS = 1e-5
RMS_EPS = 1e-6
SCALE = float(HD) ** -0.5
NOT_THERE = -1.0
TAKEN = -2.0


class Tally:

    def __init__(self, nc, ctx, name, per, credit=0):
        self.sem = ctx.enter_context(nc.semaphore(name))
        self.per, self.credit = per, credit

    def at(self, i, k):
        return i * self.per + (self.credit + k)


def stages(layer):
    C = layer["chunks"]
    first_of = layer["expert_start"]
    out = [("LN",), ("XT",), ("QK",)]
    gu = []
    for c in range(C):
        one = []
        if layer["n"] == 1:
            if c == 0:
                one.append(("BC", 0))
            one.append(("GU", c))
            if c in first_of and first_of[c] + 1 < layer["E"]:
                one.append(("BC", first_of[c] + 1))
        else:
            one.append(("GU", c))
            if c >= 1:
                one.append(("BC", c - 1))
        if c >= 2:
            one.append(("DN", c - 2))
        gu.append(one)
    if layer["n"] == 0:
        out += [("SQ",), ("VG",), *gu[0], ("MS",)]
        done = 1
    else:
        out += [("VG",)]
        done = 0
    out += [("RT",), ("CW",)]
    lead = layer["lead"]
    for c in range(done, lead):
        out += gu[c]
    done = lead
    shares = layer["shares"]
    assert lead + sum(shares) == C, (lead, shares, C)
    for r in range(G + 2):
        mine = []
        if r < G:
            mine += [((u + 0.3) / 8, [("M", r, u)]) for u in range(8)]
        if 1 <= r <= G:
            g = r - 1
            mine += [(0.12, [("NT", g)])]
            for j in range(J):
                for half in range(2):
                    st = [("E", g, j, half)]
                    if half:
                        st.append(("PV", g, j))
                    mine.append((0.4 + 0.6 * (2 * j + half) / 8, st))
        if r >= 2:
            mine += [(0.05, [("AT", r - 2)])]
        for s in range(shares[r]):
            mine.append(((s + 0.1) / shares[r], gu[done]))
            done += 1
        mine.sort(key=lambda x: x[0])
        for _, st in mine:
            out += st
    out += [("DN", C - 2), ("DN", C - 1)]
    if layer["n"] == 0:
        out += [("OT",), ("OY",)]
    out += [("YT",), ("FIN",)]
    return out


FILLS = {"XT", "QK", "VG", "MS", "CW", "BC", "GU", "M", "NT", "E", "AT", "OT", "YT"}


def layer_block(nc, layer, x_all, hbm):
    n, E, C = layer["n"], layer["E"], layer["chunks"]
    VGW = layer["vgw"]
    order = stages(layer)
    ring = {}
    for stage in order:
        if stage[0] in FILLS:
            ring[stage] = len(ring)
    uses = [sum(1 for k in ring.values() if k % SLOTS == s) for s in range(SLOTS)]

    with ExitStack() as ctx:
        def sb(name, shape, dt=F32):
            return ctx.enter_context(nc.sbuf_tensor(f"{name}_{n}", shape, dt))

        w_att = sb("w_att", [P, layer["att_cols"]])
        w_gate = sb("w_gate", [P, layer["hidden"]])
        w_up = sb("w_up", [P, layer["hidden"]])
        w_down = sb("w_down", [P, C, D])
        wq, wk = w_att[:, 0:D], w_att[:, D:2 * D]
        wvg = w_att[:, 2 * D:2 * D + VGW]
        ident = sb("ident", [P, P])
        ident_b = sb("ident_b", [P, P], BF16)
        select = sb("select", [3 * E, 8 * P], BF16)
        select_f = sb("select_f", [3 * E, 8 * P])
        if n == 0:
            wo = w_att[:, 2 * D + VGW:3 * D + VGW]
            cols = sb("cols", [P, 6])
            bias_vg = sb("bias_vg", [P, D + H])
            head_mean = sb("head_mean", [P, P])
            squares = sb("squares", [P, 2, N])
            rinv = sb("rinv", [P, 2, N])
            qk_raw = sb("qk_raw", [P, 2, N])
            gate = sb("gate", [P, J, H])
            gate_sig = sb("gate_sig", [P, J, H])
            attT = sb("attT", [P, N])
            upc = sb("upc", [P, R, N])
            rest = squares
        else:
            rest = sb("rest", [P, 2, N])
            xe = sb("xe", [P, 2, N])
            out_sb = sb("out_sb", [P, J, D])
        stats = sb("stats", [P, J, 6])
        mv = sb("mv", [P, J, 2])
        rstd = sb("rstd", [P, J])
        var_eps = sb("var_eps", [P, J])
        minus_half = sb("minus_half", [P, 1])
        xn = sb("xn", [P, J, D])
        xnT = sb("xnT", [P, N])
        qk = sb("qk", [P, 2, N])
        parts = sb("parts", [P, 3, 2, N], BF16)
        q_stack = sb("q_stack", [STACK + MAXROWS, H, N], BF16)
        k_stack = sb("k_stack", [64, H, N], BF16)
        v = sb("v", [P, J, H, VW])
        logits = sb("logits", [P, J, E])
        lmax = sb("lmax", [P, J])
        probs = sb("probs", [P, J, E + 6])
        psum_ = sb("prob_sum", [P, J])
        top8 = sb("top8", [P, J, 8])
        top2 = sb("top2", [P, J, 8])
        marked = sb("marked", [P, J, E + 6])
        cw = sb("cw", [P, J, E])
        cw_rest = sb("cw_rest", [P, J, E])
        cw_parts = sb("cw_parts", [P, J, 3, E], BF16)
        cwT = sb("cwT", [3 * E, N], BF16)
        mx = sb("mx", [P, G, HG, J])
        mx_neg = sb("mx_neg", [P, J, HG])
        mx_rest = sb("mx_rest", [P, J, HG])
        mx_parts = sb("mx_parts", [P, G, J, 3, HG], BF16)
        mxT = sb("mxT", [3 * HG, G, N], BF16)
        probsT = sb("probsT", [P, J, HG, N])
        pv_sb = sb("pv_sb", [P, 2, N])
        inv = sb("inv", [P, J, HG])
        inv2 = sb("inv2", [P, J, HG])
        att = sb("att", [P, J, D])
        th = sb("th", [P, R, N])
        up = sb("up", [P, R, N])
        act = sb("act", [P, R, N])
        hid = sb("hid", [P, R, N])
        y_sb = sb("y_sb", [P, N])

        slot = [ctx.enter_context(nc.psum_tensor(f"slot{s}_{n}", [P, 2 * BANK], F32)) for s in range(SLOTS)]
        pv_ps = ctx.enter_context(nc.psum_tensor(f"pv_ps_{n}", [P, BANK], F32))
        y_ps = ctx.enter_context(nc.psum_tensor(f"y_ps_{n}", [P, BANK], F32))

        def tally(name, per, credit=0):
            return Tally(nc, ctx, f"{name}_{n}", per, credit)

        full = [tally(f"full{s}", uses[s]) for s in range(SLOTS)]
        free = [tally(f"free{s}", uses[s], 1) for s in range(SLOTS)]
        loaded = [ctx.enter_context(nc.semaphore(f"loaded{k}_{n}")) for k in range(4)]
        consts_set = ctx.enter_context(nc.semaphore(f"consts_set_{n}"))
        sel_set = ctx.enter_context(nc.semaphore(f"sel_set_{n}"))
        carried = ctx.enter_context(nc.semaphore(f"carried_{n}"))
        ln_done = tally("ln_done", 1)
        var_done = tally("var_done", 1)
        rstd_done = tally("rstd_done", 1)
        qkraw_done = tally("qkraw_done", 1)
        sq_done = tally("sq_done", 1)
        qk_done = tally("qk_done", 2)
        hi_done = tally("hi_done", 1)
        parts_done = tally("parts_done", 1)
        parts_out = tally("parts_out", 16, 16)
        stack_in = tally("stack_in", 12 * 16)
        v_done = tally("v_done", J)
        logits_done = tally("logits_done", 1)
        gate_raw = tally("gate_raw", 1)
        gate_tanh = tally("gate_tanh", 1)
        exp_routed = tally("exp_routed", 1)
        cw_done = tally("cw_done", 1)
        cwp_done = tally("cwp_done", 1)
        actgu = tally("actgu", 2 * C)
        h_done = tally("h_done", C, R)
        h_used = tally("h_used", C, R)
        mxp_done = tally("mxp_done", G)
        mx_out = [tally(f"mx_out{g}", 16) for g in range(G)]
        mx_in = [tally(f"mx_in{g}", 16) for g in range(G)]
        p_used = tally("p_used", G * J, J)
        pv_full = tally("pv_full", G)
        pv_out = tally("pv_out", G, 1)
        y_full = tally("y_full", 1)
        y_out = tally("y_out", 1, 1)
        out_done = tally("out_done", 1)
        out_dma = tally("out_dma", 16, 16)
        dve_chain = tally("dve_chain", layer["dve_chain"])
        pool_chain = tally("pool_chain", layer["pool_chain"])

        def chunk_rows(c):
            return 96 if n == 1 and c % 3 == 2 else P

        def chunk_col(c):
            return (c // 3) * 352 + (c % 3) * P if n == 1 else c * P

        def s_of(stage):
            return ring[stage] % SLOTS

        def filled(stage):
            return full[s_of(stage)].sem

        def filled_at(i, stage):
            return full[s_of(stage)].at(i, ring[stage] // SLOTS + 1)

        def emptied(stage):
            return free[s_of(stage)].sem

        def emptied_at(i, stage):
            return free[s_of(stage)].at(i, ring[stage] // SLOTS + 1)

        def vacant_at(i, stage):
            return free[s_of(stage)].at(i, ring[stage] // SLOTS)

        def carry(eng):
            eng.sem_inc(carried, 1)

        block = ctx.enter_context(nc.Block())

        @block.sync
        def _(sp):
            if n == 0:
                sp.dma_start(x_all[:], hbm["x"].rearrange("(t p) d -> p t d", p=P)).then_inc(loaded[0], 16)
                sp.dma_start(ident[:], hbm["ident"]).then_inc(loaded[0], 16)
                sp.dma_start(cols[:], hbm["cols"]).then_inc(loaded[0], 16)
                sp.dma_start(bias_vg[:], hbm["bias_vg"].partition_broadcast(P)).then_inc(loaded[0], 16)
                sp.dma_start(head_mean[:], hbm["head_mean"]).then_inc(loaded[0], 16)
            else:
                sp.dma_start(ident[:], hbm["ident"]).then_inc(loaded[0], 16)
            sp.dma_start(w_att[:], hbm["att"]).then_inc(loaded[0], 16)
            sp.dma_start(select_f[:], hbm["select"]).then_inc(loaded[1], 16)
            sp.dma_start(w_gate[:], hbm["gate"]).then_inc(loaded[2], 16)
            sp.dma_start(w_up[:], hbm["up"]).then_inc(loaded[2], 16)
            if n == 0:
                sp.dma_start(w_down[:], hbm["down"]).then_inc(loaded[3], 16)
            else:
                for part in range(3):
                    rows = min(P, 352 - part * P)
                    sp.dma_start(w_down[0:rows, part:C:3, :],
                                 hbm["down"][:, part * P:part * P + rows, :].rearrange("e f d -> f e d"))\
                      .then_inc(loaded[3], 16)
            sp.wait_ge(consts_set, 5)
            with sp.Fori(0, B, 1) as i:
                for stage in order:
                    kind = stage[0]
                    if kind == "RT":
                        sp.wait_ge(parts_done.sem, parts_done.at(i, 1))
                        carry(sp)
                        sp.dma_start(hbm["parts"][i].rearrange("k a p t -> p (k a) t"),
                                     parts[:].rearrange("p k a t -> p (k a) t")).then_inc(parts_out.sem, 16)
                        sp.wait_ge(parts_out.sem, parts_out.at(i, 16))
                        carry(sp)
                        sp.wait_ge(p_used.sem, p_used.at(i, 0))
                        carry(sp)
                        for r, part in enumerate((0, 0, 0, 1, 1, 2)):
                            sp.dma_start(q_stack[r * HD:(r + 1) * HD, :, :],
                                         hbm["parts"][i, part, 0].rearrange("(d h) t -> d h t", h=H))\
                              .then_inc(stack_in.sem, 16)
                        for r, part in enumerate((0, 1, 2, 0, 1, 0)):
                            sp.dma_start(k_stack[r * HD:(r + 1) * HD, :, :],
                                         hbm["parts"][i, part, 1].rearrange("(d h) t -> d h t", h=H))\
                              .then_inc(stack_in.sem, 16)
                    elif kind == "NT":
                        g = stage[1]
                        sp.wait_ge(emptied(stage), emptied_at(i, stage))
                        carry(sp)
                        sp.dma_start(hbm["maxima"][i, g], mxT[:, g, :]).then_inc(mx_out[g].sem, 16)
                        sp.wait_ge(mx_out[g].sem, mx_out[g].at(i, 16))
                        carry(sp)
                        sp.dma_start(q_stack[STACK:STACK + MAXROWS, g * HG:(g + 1) * HG, :],
                                     hbm["maxima"][i, g].rearrange("(a h) t -> a h t", h=HG))\
                          .then_inc(mx_in[g].sem, 16)
                    elif kind == "FIN" and n == 1:
                        sp.wait_ge(out_done.sem, out_done.at(i, 1))
                        carry(sp)
                        sp.dma_start(hbm["out"][i].rearrange("(t p) d -> p t d", p=P), out_sb[:])\
                          .then_inc(out_dma.sem, 16)
            if n == 1:
                sp.wait_ge(out_dma.sem, out_dma.at(B - 1, 16))

        @block.tensor
        def _(pe):
            pe.wait_ge(loaded[0], 96 if n == 0 else 32)
            pe.wait_ge(consts_set, 5)
            pe.wait_ge(sel_set, 2)
            pe.wait_ge(loaded[2], 32)
            pe.wait_ge(loaded[3], 16 if n == 0 else 48)
            with pe.Fori(0, B, 1) as i:
                for stage in order:
                    kind = stage[0]
                    if stage in ring:
                        ps = slot[s_of(stage)]
                        slot_full = filled(stage)
                        pe.wait_ge(emptied(stage), vacant_at(i, stage))
                    if kind == "XT":
                        pe.wait_ge(ln_done.sem, ln_done.at(i, 1))
                        for j in range(J):
                            last = nc.tensor.transpose(ps[:, j * P:(j + 1) * P], xn[:, j, :], ident[:])
                        last.then_inc(slot_full, 1)
                    elif kind == "QK":
                        pe.wait_ge(emptied(("XT",)), emptied_at(i, ("XT",)))
                        nc.tensor.matmul(ps[:, 0:N], wq, xnT[:], start=True, stop=True)
                        nc.tensor.matmul(ps[:, BANK:BANK + N], wk, xnT[:], start=True, stop=True)\
                            .then_inc(slot_full, 1)
                    elif kind == "VG":
                        for j in range(J):
                            c0 = (j // 2) * BANK + (j % 2) * VGW
                            last = nc.tensor.matmul(ps[:, c0:c0 + VGW], xnT[:, j * P:(j + 1) * P], wvg,
                                                    start=True, stop=True)
                        last.then_inc(slot_full, 1)
                    elif kind == "MS":
                        pe.wait_ge(sq_done.sem, sq_done.at(i, 1))
                        for a in range(2):
                            last = nc.tensor.matmul(ps[:, a * BANK:a * BANK + N], head_mean[:], squares[:, a, :],
                                                    start=True, stop=True)
                        last.then_inc(slot_full, 1)
                    elif kind == "CW":
                        pe.wait_ge(cwp_done.sem, cwp_done.at(i, 1))
                        carry(pe)
                        psb = ps[:, 0:BANK].bitcast(BF16)
                        for j in range(J):
                            last = nc.tensor.transpose(psb[0:3 * E, j * P:(j + 1) * P],
                                                       cw_parts[:, j].rearrange("p a e -> p (a e)"), ident_b[:])
                        last.then_inc(slot_full, 1)
                    elif kind == "BC":
                        e = stage[1]
                        if e == 0:
                            pe.wait_ge(emptied(("CW",)), emptied_at(i, ("CW",)))
                        nc.tensor.matmul(ps[:, 0:N], select[:, e * P:(e + 1) * P], cwT[:],
                                         start=True, stop=True).then_inc(slot_full, 1)
                    elif kind == "GU":
                        c = stage[1]
                        rows, c0 = chunk_rows(c), chunk_col(c)
                        moving = xnT[:]
                        if n == 1:
                            pe.wait_ge(emptied(("BC", c // 3)), emptied_at(i, ("BC", c // 3)))
                            moving = xe[:, (c // 3) % 2, :]
                        nc.tensor.matmul(ps[0:rows, 0:N], w_gate[:, c0:c0 + rows], xnT[:], start=True, stop=True)
                        nc.tensor.matmul(ps[0:rows, BANK:BANK + N], w_up[:, c0:c0 + rows], moving,
                                         start=True, stop=True).then_inc(slot_full, 1)
                    elif kind == "DN":
                        c = stage[1]
                        rows = chunk_rows(c)
                        if c == 0:
                            pe.wait_ge(y_out.sem, y_out.at(i, 0))
                        pe.wait_ge(h_done.sem, h_done.at(i, c + 1))
                        last = nc.tensor.matmul(y_ps[:, 0:N], w_down[0:rows, c, :], hid[0:rows, c % R, :],
                                                start=(c == 0), stop=(c == C - 1 and n == 1))
                        last.then_inc(h_used.sem, 1)
                    elif kind == "M":
                        g, u = stage[1], stage[2]
                        if (g, u) == (0, 0):
                            pe.wait_ge(stack_in.sem, stack_in.at(i, 12 * 16))
                        h, j0 = g * HG + u // 2, 2 * (u % 2)
                        for a in range(2):
                            last = nc.tensor.matmul(ps[:, a * BANK:a * BANK + N],
                                                    q_stack[0:STACK, h, (j0 + a) * P:(j0 + a + 1) * P],
                                                    k_stack[0:STACK, h, :], start=True, stop=True)
                        last.then_inc(slot_full, 1)
                    elif kind == "NT":
                        g = stage[1]
                        pe.wait_ge(mxp_done.sem, mxp_done.at(i, g + 1))
                        psb = ps[:, 0:BANK].bitcast(BF16)
                        for j in range(J):
                            last = nc.tensor.transpose(psb[0:3 * HG, j * P:(j + 1) * P],
                                                       mx_parts[:, g, j].rearrange("p a h -> p (a h)"), ident_b[:])
                        last.then_inc(slot_full, 1)
                    elif kind == "E":
                        g, j, half = stage[1:]
                        if j == 0 and half == 0:
                            pe.wait_ge(mx_in[g].sem, mx_in[g].at(i, 16))
                        for a in range(2):
                            h = g * HG + 2 * half + a
                            last = nc.tensor.matmul(ps[:, a * BANK:a * BANK + N],
                                                    k_stack[0:STACK + MAXROWS, h, j * P:(j + 1) * P],
                                                    q_stack[:, h, :], start=True, stop=True)
                        last.then_inc(slot_full, 1)
                    elif kind == "PV":
                        g, j = stage[1:]
                        if (g, j) == (0, 0):
                            pe.wait_ge(v_done.sem, v_done.at(i, J))
                        if j == 0:
                            pe.wait_ge(pv_out.sem, pv_out.at(i, g))
                        pe.wait_ge(emptied(("E", g, j, 0)), emptied_at(i, ("E", g, j, 0)))
                        pe.wait_ge(emptied(("E", g, j, 1)), emptied_at(i, ("E", g, j, 1)))
                        for a in range(HG):
                            last = nc.tensor.matmul(pv_ps[a * VW:(a + 1) * VW, 0:N], v[:, j, g * HG + a, :],
                                                    probsT[:, j, a, :], start=(j == 0), stop=(j == J - 1),
                                                    skip_group_check=True)
                        last.then_inc(p_used.sem, 1)
                    elif kind == "AT":
                        g = stage[1]
                        pe.wait_ge(pv_out.sem, pv_out.at(i, g + 1 - 0))
                        for j in range(J):
                            last = nc.tensor.transpose(ps[:, j * P:(j + 1) * P],
                                                       pv_sb[:, g % 2, j * P:(j + 1) * P], ident[:])
                        last.then_inc(slot_full, 1)
                    elif kind == "OT":
                        pe.wait_ge(emptied(("AT", G - 1)), emptied_at(i, ("AT", G - 1)))
                        for j in range(J):
                            last = nc.tensor.transpose(ps[:, j * P:(j + 1) * P], att[:, j, :], ident[:])
                        last.then_inc(slot_full, 1)
                    elif kind == "OY":
                        pe.wait_ge(emptied(("OT",)), emptied_at(i, ("OT",)))
                        nc.tensor.matmul(y_ps[:, 0:N], wo, attT[:], start=False, stop=True).then_inc(y_full.sem, 1)
                    elif kind == "YT":
                        pe.wait_ge(y_out.sem, y_out.at(i, 1))
                        for j in range(J):
                            last = nc.tensor.transpose(ps[:, j * P:(j + 1) * P], y_sb[:, j * P:(j + 1) * P], ident[:])
                        last.then_inc(slot_full, 1)

        @block.scalar
        def _(sc):
            if n == 0:
                sc.wait_ge(loaded[0], 96)
            with sc.Fori(0, B, 1) as i:
                for stage in order:
                    kind = stage[0]
                    if stage in ring:
                        ps = slot[s_of(stage)]
                        slot_free = emptied(stage)
                    if kind == "XT":
                        sc.wait_ge(filled(stage), filled_at(i, stage))
                        nc.scalar.activation(xnT[:], ps[:, 0:N], ACT.Copy).then_inc(slot_free, 1)
                    elif kind == "QK":
                        sc.wait_ge(filled(stage), filled_at(i, stage))
                        if n == 0:
                            nc.scalar.activation(qk_raw[:, 0, :], ps[:, 0:N], ACT.Identity,
                                                 bias=cols[:, 0:1]).then_inc(qkraw_done.sem, 1)
                            nc.scalar.activation(qk_raw[:, 1, :], ps[:, BANK:BANK + N], ACT.Identity,
                                                 bias=cols[:, 1:2]).then_inc(slot_free, 1)
                        else:
                            nc.scalar.activation(qk[:], ps[:].rearrange("p (a t) -> p a t", a=2), ACT.Copy)\
                                .then_inc(slot_free, 1)
                            sc.wait_ge(emptied(stage), emptied_at(i, stage))
                            sc.wait_ge(parts_out.sem, parts_out.at(i, 0))
                            nc.scalar.activation(parts[:, 0], qk[:], ACT.Copy).then_inc(hi_done.sem, 1)
                    elif kind == "MS" and n == 0:
                        sc.wait_ge(filled(stage), filled_at(i, stage))
                        nc.scalar.activation(rinv[:].rearrange("p a t -> p (a t)"), ps[:], ACT.Sqrt, bias=cols[:, 5:6])\
                            .then_inc(slot_free, 1)
                        sc.wait_ge(qk_done.sem, qk_done.at(i, 2))
                        sc.wait_ge(parts_out.sem, parts_out.at(i, 0))
                        nc.scalar.activation(parts[:, 0], qk[:], ACT.Copy).then_inc(hi_done.sem, 1)
                    elif kind == "RT":
                        if n == 0:
                            sc.wait_ge(gate_raw.sem, gate_raw.at(i, 1))
                            nc.scalar.activation(gate_sig[:], gate[:], ACT.Tanh, scale=0.5)\
                                .then_inc(gate_tanh.sem, 1)
                        sc.wait_ge(logits_done.sem, logits_done.at(i, 1))
                        nc.scalar.activation(probs[:, :, 0:E], logits[:], ACT.Exp).then_inc(exp_routed.sem, 1)
                    elif kind == "CW":
                        sc.wait_ge(filled(stage), filled_at(i, stage))
                        nc.scalar.activation(cwT[:], ps[:, 0:BANK].bitcast(BF16)[0:3 * E, 0:N], ACT.Copy)\
                            .then_inc(slot_free, 1)
                    elif kind == "GU":
                        c = stage[1]
                        rows = chunk_rows(c)
                        sc.wait_ge(filled(stage), filled_at(i, stage))
                        sc.wait_ge(h_done.sem, h_done.at(i, c + 1 - R))
                        nc.scalar.activation(up[0:rows, c % R, :], ps[0:rows, BANK:BANK + N], ACT.Copy, scale=0.5)\
                            .then_inc(actgu.sem, 1)
                        nc.scalar.activation(th[0:rows, c % R, :], ps[0:rows, 0:N], ACT.Tanh, scale=0.5)\
                            .then_inc(actgu.sem, 1)
                    elif kind == "NT":
                        g = stage[1]
                        sc.wait_ge(filled(stage), filled_at(i, stage))
                        nc.scalar.activation(mxT[:, g, :], ps[:, 0:BANK].bitcast(BF16)[0:3 * HG, 0:N], ACT.Copy)\
                            .then_inc(slot_free, 1)
                    elif kind == "E":
                        g, j, half = stage[1:]
                        sc.wait_ge(filled(stage), filled_at(i, stage))
                        if half == 0:
                            sc.wait_ge(p_used.sem, p_used.at(i, g * J + j + 1 - J))
                        nc.scalar.activation(probsT[:, j, 2 * half:2 * half + 2, :],
                                             ps[:].rearrange("p (a t) -> p a t", a=2), ACT.Exp, scale=SCALE)\
                            .then_inc(slot_free, 1)
                        if j == J - 1 and half == 1:
                            sc.wait_ge(p_used.sem, p_used.at(i, (g + 1) * J))
                            nc.scalar.activation(pv_sb[:, g % 2, :], pv_ps[:], ACT.Copy).then_inc(pv_out.sem, 1)
                    elif kind == "OT":
                        sc.wait_ge(filled(stage), filled_at(i, stage))
                        nc.scalar.activation(attT[:], ps[:, 0:N], ACT.Copy).then_inc(slot_free, 1)
                    elif kind == "YT":
                        if n == 0:
                            sc.wait_ge(y_full.sem, y_full.at(i, 1))
                            nc.scalar.activation(y_sb[:], y_ps[:], ACT.Identity, bias=cols[:, 4:5])\
                                .then_inc(y_out.sem, 1)
                        else:
                            sc.wait_ge(h_used.sem, h_used.at(i, C))
                            nc.scalar.activation(y_sb[:], y_ps[:], ACT.Copy).then_inc(y_out.sem, 1)

        @block.vector
        def _(ve):
            used = [0]

            def link(i, ins, alone=False):
                used[0] += 1
                ins.then_inc(dve_chain.sem, 1)
                ve.wait_ge(dve_chain.sem, dve_chain.at(i, used[0]))
                if alone:
                    carry(ve)

            nc.vector.memset(minus_half[:], -0.5).then_inc(consts_set, 1)
            nc.vector.memset(v[:], 1.0).then_inc(consts_set, 1)
            nc.vector.memset(k_stack[32:64], 1.0).then_inc(consts_set, 1)
            nc.vector.memset(probs[:], NOT_THERE).then_inc(consts_set, 1)
            nc.vector.memset(top2[:], NOT_THERE).then_inc(consts_set, 1)
            ve.wait_ge(loaded[0], 96 if n == 0 else 32)
            nc.vector.tensor_copy(ident_b[:], ident[:]).then_inc(sel_set, 1)
            ve.wait_ge(loaded[1], 16)
            nc.vector.tensor_copy(select[:], select_f[:]).then_inc(sel_set, 1)
            ve.wait_ge(consts_set, 5)
            with ve.Fori(0, B, 1) as i:
                for stage in order:
                    kind = stage[0]
                    if stage in ring:
                        ps = slot[s_of(stage)]
                        slot_free = emptied(stage)
                    if kind == "LN":
                        for j in range(J):
                            last = nc.vector.bn_stats(stats[:, j, :], x_all[:, bass.ds(i * J + j, 1), :].rearrange("p a d -> p (a d)"))
                        link(i, last, alone=True)
                        for j in range(J):
                            last = nc.vector.bn_aggr(mv[:, j, :], stats[:, j, :])
                        link(i, last)
                        nc.vector.tensor_scalar(var_eps[:], mv[:, :, 1], LN_EPS, None, ALU.add).then_inc(var_done.sem, 1)
                        ve.wait_ge(rstd_done.sem, rstd_done.at(i, 1))
                        for j in range(J):
                            last = nc.vector.tensor_scalar(xn[:, j, :], x_all[:, bass.ds(i * J + j, 1), :].rearrange("p a d -> p (a d)"),
                                                           mv[:, j, 0:1], rstd[:, j:j + 1], ALU.subtract, ALU.mult)
                        last.then_inc(ln_done.sem, 1)
                    elif kind == "VG":
                        ve.wait_ge(filled(stage), filled_at(i, stage))
                        ve.wait_ge(p_used.sem, p_used.at(i, 0))
                        for j in range(J):
                            c0 = (j // 2) * BANK + (j % 2) * VGW
                            pv = ps[:, c0:c0 + D].rearrange("p (h d) -> p h d", h=H)
                            if n == 0:
                                ins = nc.vector.tensor_tensor(v[:, j, :, 0:HD], pv,
                                                              bias_vg[:, 0:D].rearrange("p (h d) -> p h d", h=H), ALU.add)
                            else:
                                ins = nc.vector.tensor_copy(v[:, j, :, 0:HD], pv)
                            ins.then_inc(v_done.sem, 1)
                        both = ps[:].rearrange("p (a t) -> p a t", a=2)[:, :, 0:2 * VGW].rearrange("p a (b w) -> p a b w", b=2)
                        lg4 = logits[:].rearrange("p (a b) e -> p a b e", a=2)
                        if n == 0:
                            bg = bias_vg[:, D:D + H].unsqueeze(1).unsqueeze(1).broadcast_to([P, 2, 2, H])
                            nc.vector.tensor_tensor(gate[:].rearrange("p (a b) e -> p a b e", a=2), both[:, :, :, D:D + H],
                                                    bg, ALU.add).then_inc(gate_raw.sem, 1)
                            ve.wait_ge(gate_raw.sem, gate_raw.at(i, 1))
                        nc.vector.tensor_copy(lg4, both[:, :, :, VGW - E:VGW]).then_inc(slot_free, 1)
                        ve.wait_ge(emptied(stage), emptied_at(i, stage))
                    elif kind == "MS":
                        ve.wait_ge(emptied(stage), emptied_at(i, stage))
                        link(i, nc.vector.reciprocal(rinv[:], rinv[:]))
                        for a in range(2):
                            nc.vector.scalar_tensor_tensor(out=qk[:, a, :], in0=qk_raw[:, a, :], scalar=cols[:, 2 + a:3 + a],
                                                           in1=rinv[:, a, :], op0=ALU.mult, op1=ALU.mult)\
                                .then_inc(qk_done.sem, 1)
                    elif kind == "RT":
                        link(i, nc.vector.tensor_reduce(lmax[:], logits[:], AXIS.X, ALU.max))
                        nc.vector.tensor_tensor(logits[:], logits[:], lmax[:].unsqueeze(2).broadcast_to([P, J, E]),
                                                ALU.subtract).then_inc(logits_done.sem, 1)
                        p = probs[:, :, 0:E]
                        ve.wait_ge(exp_routed.sem, exp_routed.at(i, 1))
                        link(i, nc.vector.tensor_reduce(psum_[:], p, AXIS.X, ALU.add))
                        link(i, nc.vector.reciprocal(psum_[:], psum_[:]))
                        link(i, nc.vector.tensor_tensor(p, p, psum_[:].unsqueeze(2).broadcast_to([P, J, E]), ALU.mult),
                             alone=True)
                        for j in range(J):
                            last = nc.vector.max(top8[:, j, :], probs[:, j, 0:E])
                        link(i, last)
                        link(i, nc.vector.tensor_copy(top2[:, :, 0:2], top8[:, :, 0:2]), alone=True)
                        for j in range(J):
                            last = nc.vector.match_replace(marked[:, j, :], top2[:, j, :], probs[:, j, :], TAKEN)
                        link(i, last)
                        c_in = nc.vector.scalar_tensor_tensor(out=cw[:], in0=marked[:, :, 0:E], scalar=(NOT_THERE + TAKEN) / 2,
                                                              in1=p, op0=ALU.is_lt, op1=ALU.mult)
                        if n == 0:
                            c_in.then_inc(cw_done.sem, 1)
                            ve.wait_ge(gate_tanh.sem, gate_tanh.at(i, 1))
                            link(i, nc.vector.tensor_scalar(gate_sig[:], gate_sig[:], 1.0, 0.5, ALU.add, ALU.mult))
                        else:
                            link(i, c_in)
                            link(i, nc.vector.tensor_tensor(psum_[:], top8[:, :, 0], top8[:, :, 1], ALU.add))
                            link(i, nc.vector.tensor_scalar(psum_[:], psum_[:], 1e-20, None, ALU.add))
                            link(i, nc.vector.reciprocal(psum_[:], psum_[:]))
                            nc.vector.tensor_tensor(cw[:], cw[:], psum_[:].unsqueeze(2).broadcast_to([P, J, E]), ALU.mult)\
                                .then_inc(cw_done.sem, 1)
                    elif kind == "BC":
                        e = stage[1]
                        ve.wait_ge(filled(stage), filled_at(i, stage))
                        if n == 1:
                            nc.vector.tensor_tensor(xe[:, e % 2, :], xnT[:], ps[:, 0:N], ALU.mult).then_inc(slot_free, 1)
                        else:
                            c = e + 1
                            ve.wait_ge(h_done.sem, h_done.at(i, c + 1 - R))
                            nc.vector.tensor_tensor(upc[:, c % R, :], up[:, c % R, :], ps[:, 0:N], ALU.mult)\
                                .then_inc(slot_free, 1)
                    elif kind == "GU":
                        c = stage[1]
                        rows = chunk_rows(c)
                        ve.wait_ge(actgu.sem, actgu.at(i, 2 * (c + 1)))
                        ve.wait_ge(h_done.sem, h_done.at(i, c + 1 - R))
                        ve.wait_ge(filled(stage), filled_at(i, stage))
                        nc.vector.scalar_tensor_tensor(out=act[0:rows, c % R, :], in0=th[0:rows, c % R, :], scalar=1.0,
                                                       in1=ps[0:rows, 0:N], op0=ALU.add, op1=ALU.mult)\
                            .then_inc(slot_free, 1)
                    elif kind == "M":
                        g, u = stage[1], stage[2]
                        hh, j0 = u // 2, 2 * (u % 2)
                        ve.wait_ge(filled(stage), filled_at(i, stage))
                        nc.vector.tensor_reduce(mx[:, g, hh, j0:j0 + 2], ps[:].rearrange("p (a t) -> p a t", a=2),
                                                AXIS.X, ALU.max).then_inc(slot_free, 1)
                    elif kind == "AT":
                        g = stage[1]
                        ve.wait_ge(filled(stage), filled_at(i, stage))
                        src = ps[:, 0:N].rearrange("p (j h c) -> p j h c", j=J, h=HG)
                        link(i, nc.vector.reciprocal(inv[:], src[:, :, :, HD]))
                        use = inv
                        if n == 0:
                            link(i, nc.vector.tensor_tensor(inv2[:], inv[:], gate_sig[:, :, g * HG:(g + 1) * HG], ALU.mult))
                            use = inv2
                        dst = att[:, :, g * HG * HD:(g + 1) * HG * HD].rearrange("p j (h d) -> p j h d", h=HG)
                        nc.vector.tensor_tensor(dst, src[:, :, :, 0:HD], use[:].unsqueeze(3).broadcast_to([P, J, HG, HD]),
                                                ALU.mult).then_inc(slot_free, 1)
                    elif kind == "YT":
                        ve.wait_ge(filled(stage), filled_at(i, stage))
                        xs = x_all[:, bass.ds(i * J, J), :]
                        y = ps[:, 0:N].rearrange("p (j d) -> p j d", j=J)
                        if n == 0:
                            nc.vector.tensor_tensor(xs, xs, y, ALU.add).then_inc(slot_free, 1)
                        else:
                            ve.wait_ge(out_dma.sem, out_dma.at(i, 0))
                            nc.vector.tensor_tensor(out_sb[:], xs, y, ALU.add).then_inc(slot_free, 1)
                            ve.wait_ge(emptied(stage), emptied_at(i, stage))
                            nc.vector.tensor_tensor(out_sb[:], out_sb[:], att[:], ALU.add).then_inc(out_done.sem, 1)
            assert used[0] == dve_chain.per, (n, "dve", used)

        @block.gpsimd
        def _(gp):
            used = [0]

            def link(i, ins):
                used[0] += 1
                ins.then_inc(pool_chain.sem, 1)
                gp.wait_ge(pool_chain.sem, pool_chain.at(i, used[0]))
                carry(gp)

            for t in (*free, parts_out, h_done, h_used, p_used, pv_out, y_out, out_dma):
                gp.sem_inc(t.sem, t.credit)
            gp.wait_ge(consts_set, 5)
            with gp.Fori(0, B, 1) as i:
                for stage in order:
                    kind = stage[0]
                    if kind == "LN":
                        gp.wait_ge(var_done.sem, var_done.at(i, 1))
                        nc.gpsimd.tensor_tensor(rstd[:], var_eps[:], minus_half[:].broadcast_to([P, J]), ALU.pow)\
                            .then_inc(rstd_done.sem, 1)
                    elif kind == "SQ":
                        gp.wait_ge(qkraw_done.sem, qkraw_done.at(i, 1))
                        gp.wait_ge(emptied(("QK",)), emptied_at(i, ("QK",)))
                        nc.gpsimd.tensor_tensor(squares[:], qk_raw[:], qk_raw[:], ALU.mult).then_inc(sq_done.sem, 1)
                    elif kind == ("MS" if n == 0 else "QK"):
                        if n == 0:
                            gp.wait_ge(qk_done.sem, qk_done.at(i, 2))
                        else:
                            gp.wait_ge(emptied(stage), emptied_at(i, stage))
                        gp.wait_ge(hi_done.sem, hi_done.at(i, 1))
                        link(i, nc.gpsimd.tensor_tensor(rest[:], qk[:], parts[:, 0], ALU.subtract))
                        link(i, nc.gpsimd.tensor_tensor(parts[:, 1], qk[:], parts[:, 0], ALU.subtract))
                        nc.gpsimd.tensor_tensor(parts[:, 2], rest[:], parts[:, 1], ALU.subtract)\
                            .then_inc(parts_done.sem, 1)
                    elif kind == "RT":
                        gp.wait_ge(cw_done.sem, cw_done.at(i, 1))
                        carry(gp)
                        link(i, nc.gpsimd.tensor_copy(cw_parts[:, :, 0, :], cw[:]))
                        link(i, nc.gpsimd.tensor_tensor(cw_rest[:], cw[:], cw_parts[:, :, 0, :], ALU.subtract))
                        link(i, nc.gpsimd.tensor_copy(cw_parts[:, :, 1, :], cw_rest[:]))
                        nc.gpsimd.tensor_tensor(cw_parts[:, :, 2, :], cw_rest[:], cw_parts[:, :, 1, :], ALU.subtract)\
                            .then_inc(cwp_done.sem, 1)
                    elif kind == "GU":
                        c = stage[1]
                        rows = chunk_rows(c)
                        if n == 1 or c == 0:
                            gp.wait_ge(emptied(("GU", c)), emptied_at(i, ("GU", c)))
                            gp.wait_ge(h_used.sem, h_used.at(i, c + 1 - R))
                            nc.gpsimd.tensor_tensor(hid[0:rows, c % R, :], act[0:rows, c % R, :], up[0:rows, c % R, :],
                                                    ALU.mult).then_inc(h_done.sem, 1)
                    elif kind == "BC" and n == 0:
                        c = stage[1] + 1
                        gp.wait_ge(emptied(("GU", c)), emptied_at(i, ("GU", c)))
                        gp.wait_ge(emptied(stage), emptied_at(i, stage))
                        gp.wait_ge(h_used.sem, h_used.at(i, c + 1 - R))
                        nc.gpsimd.tensor_tensor(hid[:, c % R, :], act[:, c % R, :], upc[:, c % R, :],
                                                ALU.mult).then_inc(h_done.sem, 1)
                    elif kind == "M" and stage[2] == 7:
                        g = stage[1]
                        for u in range(8):
                            if all(s_of(("M", g, w)) != s_of(("M", g, u)) for w in range(u + 1, 8)):
                                gp.wait_ge(emptied(("M", g, u)), emptied_at(i, ("M", g, u)))
                        carry(gp)
                        hi, mid, lo = (mx_parts[:, g, :, a, :] for a in range(3))
                        link(i, nc.gpsimd.tensor_scalar(mx_neg[:], mx[:, g].rearrange("p h j -> p j h"), -1.0, None, ALU.mult))
                        link(i, nc.gpsimd.tensor_copy(hi, mx_neg[:]))
                        link(i, nc.gpsimd.tensor_tensor(mx_rest[:], mx_neg[:], hi, ALU.subtract))
                        link(i, nc.gpsimd.tensor_copy(mid, mx_rest[:]))
                        nc.gpsimd.tensor_tensor(lo, mx_rest[:], mid, ALU.subtract).then_inc(mxp_done.sem, 1)
            assert used[0] == pool_chain.per, (n, "pool", used)


def layers():
    return (
        {"n": 0, "E": 16, "chunks": 9, "hidden": 9 * P, "vgw": D + H + 16, "att_cols": 2 * D + (D + H + 16) + D,
         "expert_start": {}, "lead": 2, "shares": (2, 1, 1, 1, 2, 0), "dve_chain": 19, "pool_chain": 21},
        {"n": 1, "E": 8, "chunks": 24, "hidden": 8 * 352, "vgw": D + 8, "att_cols": 2 * D + (D + 8),
         "expert_start": {3 * e: e for e in range(8)}, "lead": 3, "shares": (6, 4, 4, 3, 3, 1), "dve_chain": 17,
         "pool_chain": 21},
    )


def two_layers(nc, h0, h1):
    with ExitStack() as ctx:
        x_all = ctx.enter_context(nc.sbuf_tensor("x_all", [P, B * J, D], F32))
        l0, l1 = layers()
        layer_block(nc, l0, x_all, h0)
        layer_block(nc, l1, x_all, h1)


def kernel(**inputs):
    import numpy as np
    import concourse.bacc as bacc
    from concourse.bass_utils import run_bass_kernel_spmd

    x = {k: np.asarray(a) for k, a in inputs.items()}
    by_d = np.arange(D).reshape(H, HD).T.reshape(D)
    per_d = np.repeat(np.arange(HD), H)
    f0, f1 = x["L0_ffn_Wg"], x["L1_ffn_W1"]

    def side(a):
        return np.transpose(a, (1, 0, 2)).reshape(D, -1)

    wq0 = x["L0_attn_Wq"]
    eye = np.eye(P, dtype=np.float32)
    sel0 = np.zeros((3, 16, 8, P), np.float32)
    sel1 = np.zeros((3, 8, 8, P), np.float32)
    for c in range(8):
        sel0[:, 2 * c, c, 0:64] = 1.0
        sel0[:, 2 * c + 1, c, 64:128] = 1.0
        sel1[:, c, c, :] = 1.0
    head_mean = (np.arange(P)[:, None] % H == np.arange(P)[None] % H).astype(np.float32) / HD
    arrays0 = {
        "x": x["L0_attn_x"].reshape(B * N, D),
        "ident": eye,
        "select": sel0.reshape(48, 8 * P),
        "head_mean": head_mean,
        "cols": np.stack([x["L0_attn_bq"][:D][by_d], x["L0_attn_bk"][by_d], x["L0_attn_qn_w"][per_d],
                          x["L0_attn_kn_w"][per_d], x["L0_attn_bo"], np.full(D, RMS_EPS, np.float32)], axis=1),
        "bias_vg": np.concatenate([x["L0_attn_bv"], x["L0_attn_bq"][D:]]),
        "att": np.concatenate([wq0[:, :D][:, by_d], x["L0_attn_Wk"][:, by_d], x["L0_attn_Wv"], wq0[:, D:],
                               x["L0_ffn_Wr"], x["L0_attn_Wo"]], axis=1),
        "gate": np.concatenate([x["L0_ffn_Sg"], side(x["L0_ffn_Wg"])], axis=1),
        "up": np.concatenate([x["L0_ffn_Su"], side(x["L0_ffn_Wu"])], axis=1),
        "down": np.concatenate([x["L0_ffn_Sd"][None], x["L0_ffn_Wd"].reshape(8, P, D)]).transpose(1, 0, 2),
    }
    arrays1 = {
        "ident": eye,
        "select": sel1.reshape(24, 8 * P),
        "att": np.concatenate([x["L1_attn_Wq"].T[:, by_d], x["L1_attn_Wk"].T[:, by_d], x["L1_attn_Wv"].T,
                               x["L1_ffn_Wg"].T], axis=1),
        "gate": side(np.transpose(x["L1_ffn_W1"], (0, 2, 1))),
        "up": side(np.transpose(x["L1_ffn_W3"], (0, 2, 1))),
        "down": np.transpose(x["L1_ffn_W2"], (0, 2, 1)),
    }
    nc = bacc.Bacc("TRN2", target_bir_lowering=False, num_devices=1)
    given, hbm = {}, []
    for n, arrays in enumerate((arrays0, arrays1)):
        aps = {}
        for name, a in arrays.items():
            a = np.ascontiguousarray(a)
            full = f"in{n}_{name}"
            given[full] = a
            aps[name] = nc.dram_tensor(full, a.shape, mybir.dt.from_np(a.dtype), kind="ExternalInput").ap()
        aps["parts"] = nc.dram_tensor(f"parts{n}", (B, 3, 2, P, N), BF16, kind="Internal").ap()
        aps["maxima"] = nc.dram_tensor(f"maxima{n}", (B, G, 3 * HG, N), BF16, kind="Internal").ap()
        hbm.append(aps)
    hbm[1]["out"] = nc.dram_tensor("out", (B, N, D), F32, kind="ExternalOutput").ap()
    two_layers(nc, hbm[0], hbm[1])
    r = run_bass_kernel_spmd(nc, [given], core_ids=[0])
    return r.results[0]["out"]
```

```python
import concourse.bass as bass
from concourse import mybir
from contextlib import ExitStack
import struct

F32 = mybir.dt.float32
BF16 = mybir.dt.bfloat16
ACT = mybir.ActivationFunctionType
ALU = mybir.AluOpType
AXIS = mybir.AxisListType

B, N, D = 4, 512, 128
H, HD = 16, 8
P = 128
J = N // P
G, HG = 4, 4
VW = 32
STACK = 9 * HD
MAXROWS = 3
SLOTS = 3
BANK = 512
R = 3
LN_EPS = 1e-5
RMS_EPS = 1e-6
SCALE = float(HD) ** -0.5
TWO_ONES = struct.unpack("<f", b"\x80\x3f\x80\x3f")[0]
NOT_THERE = -1.0
TAKEN = -2.0


class Tally:

    def __init__(self, nc, ctx, name, per, credit=0):
        self.sem = ctx.enter_context(nc.semaphore(name))
        self.per, self.credit = per, credit

    def at(self, i, k):
        return i * self.per + (self.credit + k)

    def next(self, i, k):
        return i * self.per + (self.per + self.credit + k)


def stages(layer, main, setup):
    C = layer["chunks"]
    at = []

    def put(time, *found):
        at.append((time, len(at), found))

    if main:
        put(0.0, ("CW",))
        for g in range(G):
            if g >= 1:
                for u in range(8):
                    put(g - 1 + (u + 0.3) / 8, ("M", g, u))
            put(g + 0.12, ("NT", g))
            for j in range(J):
                for half in range(2):
                    put(g + 0.4 + 0.6 * (2 * j + half) / 8, ("E", g, j, half))
                put(g + 0.4 + 0.6 * (2 * j + 3.1) / 8, ("PV", g, j))
            put(g + 1.12, ("PO", g))
            put(g + 1.2, ("AT", g))
        span = layer["span"]
        for c in range(C):
            time = span * (c + 0.3) / C
            if layer["n"] == 1:
                if c == 0:
                    put(time - 0.01, ("BC", 0))
                put(time, ("GU", c))
                put(time + layer["gate"], ("GA", c))
                if c % 3 == 0 and c // 3 + 1 < layer["E"]:
                    put(time + 0.001, ("BC", c // 3 + 1))
            else:
                put(time, ("GU", c))
                put(time + layer["gate"], ("GA", c))
                if c >= 1:
                    put(time + layer["gate"] + 0.001, ("BC", c - 1))
            put(min(time + layer["lag"] * span / C, span + 0.05 + 0.001 * c), ("DN", c))
        if layer["n"] == 0:
            put(4.45, ("OT",))
            put(4.6, ("OY",))
        put(4.8, ("YT",))
    if setup:
        put(0.1, ("LN",))
        put(0.25, ("XN",))
        put(0.4, ("XT",))
        put(0.5, ("QK",))
        if layer["n"] == 0:
            put(0.55, ("SQ",))
            put(0.8, ("MS",))
            for k in range(4):
                put(0.9 + 0.15 * k, ("RC", k))
            put(1.5, ("QN",))
        put(1.55, ("HI",))
        put(1.7, ("PT",))
        put(2.2, ("RF", 0))
        put(2.4, ("RF", 1))
        put(3.3, ("RF", 2))
        put(4.3, ("RF", 3))
        for u in range(8):
            put(3 + (u + 0.3) / 8, ("M", 0, u))
        values = layer["values"] if main else 1.6
        put(values, ("VG",))
        put(values + 0.05, ("RT",))
        put(values + 0.3, ("RW",))
        put(4.4, ("HAND",))
    return [stage for _, _, found in sorted(at) for stage in found]


class Phase:

    def __init__(self, layer, main, setup, before=None):
        self.main, self.setup = main, setup
        self.order = stages(layer, main, setup)
        self.uses = [0] * SLOTS
        self.ring, self.nth = {}, {}
        idle = [0.0] * SLOTS
        now = 0.0
        for stage in self.order:
            if stage[0] in FILLS:
                takes, stays = FILLS[stage[0]]
                s = len(self.ring) % SLOTS
                now = max(now, idle[s]) + takes
                idle[s] = now + stays
                self.ring[stage] = s
                self.nth[stage] = self.uses[s]
                self.uses[s] += 1
        self.base = [0] * SLOTS
        self.per = [0] * SLOTS
        self.links = {e: layer["links"][e][0] * setup + layer["links"][e][1] * main for e in ("dve", "pool")}
        self.link_base = {"dve": 0, "pool": 0}
        self.link_per = {"dve": 0, "pool": 0}

    def follow(self, first, turn):
        self.base, self.per = first.uses, turn.uses
        self.link_base, self.link_per = first.links, turn.links
        return self

    def slot(self, stage):
        return self.ring[stage]

    def same(self, a, b):
        return self.slot(a) == self.slot(b)

    def count(self, i, stage):
        s = self.slot(stage)
        return i * self.per[s] + (self.base[s] + self.nth[stage]) if self.per[s] else self.nth[stage]

    def link(self, i, engine, k):
        return i * self.link_per[engine] + (self.link_base[engine] + k) if self.link_per[engine] else k


FILLS = {"XT": (1.0, 1.0), "QK": (1.8, 1.5), "VG": (1.2, 2.0), "MS": (1.8, 1.5), "CW": (0.4, 0.6), "BC": (0.3, 1.0),
         "GU": (1.8, 2.4), "M": (0.5, 1.4), "NT": (0.4, 0.6), "E": (0.5, 1.4), "AT": (1.0, 1.5), "OT": (1.0, 1.0),
         "YT": (1.0, 1.0)}


def layer_block(nc, layer, x_all, hbm):
    n, E, C = layer["n"], layer["E"], layer["chunks"]
    VGW = layer["vgw"]
    first = Phase(layer, False, True)
    body = Phase(layer, True, True)
    body.follow(first, body)
    last = Phase(layer, True, False).follow(first, body)

    with ExitStack() as ctx:
        def sb(name, shape, dt=F32):
            return ctx.enter_context(nc.sbuf_tensor(f"{name}_{n}", shape, dt))

        w_att = sb("w_att", [P, layer["att_cols"]])
        w_gate = sb("w_gate", [P, layer["hidden"]])
        w_up = sb("w_up", [P, layer["hidden"]])
        w_down = sb("w_down", [P, C, D])
        wq, wk = w_att[:, 0:D], w_att[:, D:2 * D]
        wvg = w_att[:, 2 * D:2 * D + VGW]
        ident = sb("ident", [P, P])
        ident_b = sb("ident_b", [P, P], BF16)
        select = sb("select", [3 * E, 8 * P], BF16)
        select_f = sb("select_f", [3 * E, 8 * P])
        if n == 0:
            wo = w_att[:, 2 * D + VGW:3 * D + VGW]
            cols = sb("cols", [P, 6])
            bias_vg = sb("bias_vg", [P, D + H])
            head_mean = sb("head_mean", [P, P])
            squares = sb("squares", [P, 2, N])
            rinv = sb("rinv", [P, 2, N])
            qk_raw = sb("qk_raw", [P, 2, N])
            gate = sb("gate", [P, J, H])
            gate_sig = sb("gate_sig", [P, J, H])
            attT = sb("attT", [P, N])
            upc = sb("upc", [P, R, N])
            rest = squares
        else:
            rest = sb("rest", [P, 2, N])
            xe = sb("xe", [P, 2, N])
            out_sb = sb("out_sb", [P, J, D])
        stats = sb("stats", [P, J, 6])
        mv = sb("mv", [P, J, 2])
        rstd = sb("rstd", [P, J])
        var_eps = sb("var_eps", [P, J])
        minus_half = sb("minus_half", [P, 1])
        xn = sb("xn", [P, J, D])
        xnT = sb("xnT", [P, N])
        qk = sb("qk", [P, 2, N])
        parts = sb("parts", [P, 2, 3, N], BF16)
        q_stack = sb("q_stack", [STACK + MAXROWS, H, N], BF16)
        k_stack = sb("k_stack", [96, H, N], BF16)
        v_next = sb("v_next", [P, J, D])
        xnT_next = sb("xnT_next", [P, N])
        v = sb("v", [P, J, H, VW])
        logits = sb("logits", [P, J, E])
        lmax = sb("lmax", [P, J])
        probs = sb("probs", [P, J, E + 6])
        psum_ = sb("prob_sum", [P, J])
        top8 = sb("top8", [P, J, 8])
        top2 = sb("top2", [P, J, 8])
        marked = sb("marked", [P, J, E + 6])
        cw = sb("cw", [P, J, E])
        cw_rest = sb("cw_rest", [P, J, E])
        cw_parts = sb("cw_parts", [P, J, 3, E], BF16)
        cwT = sb("cwT", [3 * E, N], BF16)
        mx = sb("mx", [P, G, HG, J])
        mx_neg = sb("mx_neg", [P, J, HG])
        mx_rest = sb("mx_rest", [P, J, HG])
        mx_parts = sb("mx_parts", [P, G, J, 3, HG], BF16)
        mxT = sb("mxT", [3 * HG, G, N], BF16)
        probsT = sb("probsT", [P, J, HG, N])
        pv_sb = sb("pv_sb", [P, 2, N])
        inv = sb("inv", [P, J, HG])
        inv2 = sb("inv2", [P, J, HG])
        att = sb("att", [P, J, D])
        th = sb("th", [P, R, N])
        up = sb("up", [P, R, N])
        act = sb("act", [P, R, N])
        hid = sb("hid", [P, R, N])
        y_sb = sb("y_sb", [P, N])

        slot = [ctx.enter_context(nc.psum_tensor(f"slot{s}_{n}", [P, 2 * BANK], F32)) for s in range(SLOTS)]
        pv_ps = ctx.enter_context(nc.psum_tensor(f"pv_ps_{n}", [P, BANK], F32))
        y_ps = ctx.enter_context(nc.psum_tensor(f"y_ps_{n}", [P, BANK], F32))

        def tally(name, per, credit=0):
            return Tally(nc, ctx, f"{name}_{n}", per, credit)

        full = [tally(f"full{s}", 0) for s in range(SLOTS)]
        free = [tally(f"free{s}", 0, 1) for s in range(SLOTS)]
        loaded = [ctx.enter_context(nc.semaphore(f"loaded{k}_{n}")) for k in range(4)]
        consts_set = ctx.enter_context(nc.semaphore(f"consts_set_{n}"))
        ones_set = ctx.enter_context(nc.semaphore(f"ones_set_{n}"))
        sel_set = ctx.enter_context(nc.semaphore(f"sel_set_{n}"))
        carried = ctx.enter_context(nc.semaphore(f"carried_{n}"))
        ln_done = tally("ln_done", 1)
        var_done = tally("var_done", 1)
        rstd_done = tally("rstd_done", 1)
        qkraw_done = tally("qkraw_done", 1)
        sq_done = tally("sq_done", 1)
        qk_done = tally("qk_done", 2)
        hi_done = tally("hi_done", 1)
        parts_done = tally("parts_done", 1)
        parts_out = tally("parts_out", 16, 16)
        stack_in = [tally(f"stack_in{g}", 6 * 16) for g in range(G)]
        hand_done = tally("hand_done", 1)
        hand_v_done = tally("hand_v_done", 1)
        rc_done = tally("rc_done", 4)
        logits_done = tally("logits_done", 1)
        gate_raw = tally("gate_raw", 1)
        gate_tanh = tally("gate_tanh", 1)
        exp_routed = tally("exp_routed", 1)
        cw_done = tally("cw_done", 1)
        cwp_done = tally("cwp_done", 1)
        actgu = tally("actgu", 2 * C)
        h_done = tally("h_done", C, R)
        h_used = tally("h_used", C, R)
        mxp_done = tally("mxp_done", G)
        mx_out = [tally(f"mx_out{g}", 16) for g in range(G)]
        mx_in = [tally(f"mx_in{g}", 16) for g in range(G)]
        p_used = tally("p_used", G * J, J)
        pv_full = tally("pv_full", G)
        pv_out = tally("pv_out", G, 1)
        y_full = tally("y_full", 1)
        y_out = tally("y_out", 1, 1)
        out_done = tally("out_done", 1)
        out_dma = tally("out_dma", 16, 16)
        dve_chain = tally("dve_chain", 0)
        pool_chain = tally("pool_chain", 0)

        def chunk_rows(c):
            return 96 if n == 1 and c % 3 == 2 else P

        def chunk_col(c):
            return (c // 3) * 352 + (c % 3) * P if n == 1 else c * P

        def filled(ph, stage):
            return full[ph.slot(stage)].sem

        def filled_at(ph, i, stage):
            return ph.count(i, stage) + 1

        def emptied(ph, stage):
            return free[ph.slot(stage)].sem

        def emptied_at(ph, i, stage):
            return ph.count(i, stage) + 2

        def vacant_at(ph, i, stage):
            return ph.count(i, stage) + 1

        def carry(eng):
            eng.sem_inc(carried, 1)

        block = ctx.enter_context(nc.Block())

        @block.sync
        def _(sp):
            if n == 0:
                sp.dma_start(x_all[:], hbm["x"].rearrange("(t p) d -> p t d", p=P)).then_inc(loaded[0], 16)
                sp.dma_start(ident[:], hbm["ident"]).then_inc(loaded[0], 16)
                sp.dma_start(cols[:], hbm["cols"]).then_inc(loaded[0], 16)
                sp.dma_start(bias_vg[:], hbm["bias_vg"].partition_broadcast(P)).then_inc(loaded[0], 16)
                sp.dma_start(head_mean[:], hbm["head_mean"]).then_inc(loaded[0], 16)
            else:
                sp.dma_start(ident[:], hbm["ident"]).then_inc(loaded[0], 16)
            sp.dma_start(w_att[:], hbm["att"]).then_inc(loaded[0], 16)
            sp.dma_start(select_f[:], hbm["select"]).then_inc(loaded[1], 16)
            sp.dma_start(w_gate[:], hbm["gate"]).then_inc(loaded[2], 16)
            sp.dma_start(w_up[:], hbm["up"]).then_inc(loaded[2], 16)
            if n == 0:
                sp.dma_start(w_down[:], hbm["down"]).then_inc(loaded[3], 16)
            else:
                for part in range(3):
                    rows = min(P, 352 - part * P)
                    sp.dma_start(w_down[0:rows, part:C:3, :],
                                 hbm["down"][:, part * P:part * P + rows, :].rearrange("e f d -> f e d"))\
                      .then_inc(loaded[3], 16)
            sp.wait_ge(ones_set, 1)
            def turn(ph, i):
                for stage in ph.order:
                    kind = stage[0]
                    if kind == "RF":
                        g = stage[1]
                        if g == 0:
                            sp.wait_ge(parts_done.sem, parts_done.next(i, 1))
                            carry(sp)
                            sp.dma_start(hbm["parts"][i + 1].rearrange("a k p t -> p (a k) t"),
                                         parts[:].rearrange("p a k t -> p (a k) t")).then_inc(parts_out.sem, 16)
                            sp.wait_ge(parts_out.sem, parts_out.next(i, 16))
                            carry(sp)
                        if ph.main:
                            sp.wait_ge(p_used.sem, p_used.at(i, (g + 1) * J))
                            carry(sp)
                        heads = slice(g * HG, (g + 1) * HG)
                        q_rows = hbm["parts"][i + 1, 0].rearrange("k (d h) t -> (k d) h t", h=H)[:, heads, :]
                        for b in range(3):
                            sp.dma_start(q_stack[b * 3 * HD:(b + 1) * 3 * HD, heads, :], q_rows)\
                              .then_inc(stack_in[g].sem, 16)
                            k_rows = hbm["parts"][i + 1, 1, b].rearrange("(d h) t -> d h t", h=H)[:, heads, :]
                            sp.dma_start(k_stack[b * 3 * HD:(b + 1) * 3 * HD, heads, :],
                                         k_rows.unsqueeze(0).broadcast_to([3, HD, HG, N]))\
                              .then_inc(stack_in[g].sem, 16)
                    elif kind == "NT":
                        g = stage[1]
                        sp.wait_ge(emptied(ph, stage), emptied_at(ph, i, stage))
                        carry(sp)
                        sp.dma_start(hbm["maxima"][i, g], mxT[:, g, :]).then_inc(mx_out[g].sem, 16)
                        sp.wait_ge(mx_out[g].sem, mx_out[g].at(i, 16))
                        carry(sp)
                        sp.dma_start(q_stack[STACK:STACK + MAXROWS, g * HG:(g + 1) * HG, :],
                                     hbm["maxima"][i, g].rearrange("(a h) t -> a h t", h=HG))\
                          .then_inc(mx_in[g].sem, 16)
                    elif kind == "YT" and n == 1:
                        sp.wait_ge(out_done.sem, out_done.at(i, 1))
                        carry(sp)
                        sp.dma_start(hbm["out"][i].rearrange("(t p) d -> p t d", p=P), out_sb[:])\
                          .then_inc(out_dma.sem, 16)

            turn(first, -1)
            with sp.Fori(0, B - 1, 1) as i:
                turn(body, i)
            turn(last, B - 1)
            if n == 1:
                sp.wait_ge(out_dma.sem, out_dma.at(B - 1, 16))

        @block.tensor
        def _(pe):
            pe.wait_ge(loaded[0], 96 if n == 0 else 32)
            pe.wait_ge(consts_set, 4)
            pe.wait_ge(sel_set, 1)
            def turn(ph, i):
                for stage in ph.order:
                    kind = stage[0]
                    if stage in ph.ring:
                        ps = slot[ph.slot(stage)]
                        slot_full = filled(ph, stage)
                        pe.wait_ge(emptied(ph, stage), vacant_at(ph, i, stage))
                    if kind == "XT":
                        pe.wait_ge(ln_done.sem, ln_done.next(i, 1))
                        for j in range(J):
                            last = nc.tensor.transpose(ps[:, j * P:(j + 1) * P], xn[:, j, :], ident[:])
                        last.then_inc(slot_full, 1)
                    elif kind == "QK":
                        if not ph.same(stage, ("XT",)):
                            pe.wait_ge(emptied(ph, ("XT",)), emptied_at(ph, i, ("XT",)))
                        nc.tensor.matmul(ps[:, 0:N], wq, xnT_next[:], start=True, stop=True)
                        nc.tensor.matmul(ps[:, BANK:BANK + N], wk, xnT_next[:], start=True, stop=True)\
                            .then_inc(slot_full, 1)
                    elif kind == "VG":
                        for j in range(J):
                            c0 = (j // 2) * BANK + (j % 2) * VGW
                            last = nc.tensor.matmul(ps[:, c0:c0 + VGW], xnT_next[:, j * P:(j + 1) * P], wvg,
                                                    start=True, stop=True)
                        last.then_inc(slot_full, 1)
                    elif kind == "MS":
                        pe.wait_ge(sq_done.sem, sq_done.next(i, 1))
                        for a in range(2):
                            last = nc.tensor.matmul(ps[:, a * BANK:a * BANK + N], head_mean[:], squares[:, a, :],
                                                    start=True, stop=True)
                        last.then_inc(slot_full, 1)
                    elif kind == "CW":
                        pe.wait_ge(cwp_done.sem, cwp_done.at(i, 1))
                        carry(pe)
                        psb = ps[:, 0:BANK].bitcast(BF16)
                        for j in range(J):
                            last = nc.tensor.transpose(psb[0:3 * E, j * P:(j + 1) * P],
                                                       cw_parts[:, j].rearrange("p a e -> p (a e)"), ident_b[:])
                        last.then_inc(slot_full, 1)
                    elif kind == "BC":
                        e = stage[1]
                        if e == 0 and not ph.same(stage, ("CW",)):
                            pe.wait_ge(emptied(ph, ("CW",)), emptied_at(ph, i, ("CW",)))
                        nc.tensor.matmul(ps[:, 0:N], select[:, e * P:(e + 1) * P], cwT[:],
                                         start=True, stop=True).then_inc(slot_full, 1)
                    elif kind == "GU":
                        c = stage[1]
                        rows, c0 = chunk_rows(c), chunk_col(c)
                        if c == 0:
                            pe.wait_ge(hand_done.sem, hand_done.at(i, 1))
                        moving = xnT[:]
                        if n == 1:
                            if not ph.same(stage, ("BC", c // 3)):
                                pe.wait_ge(emptied(ph, ("BC", c // 3)), emptied_at(ph, i, ("BC", c // 3)))
                            moving = xe[:, (c // 3) % 2, :]
                        nc.tensor.matmul(ps[0:rows, 0:N], w_gate[:, c0:c0 + rows], xnT[:], start=True, stop=True)
                        nc.tensor.matmul(ps[0:rows, BANK:BANK + N], w_up[:, c0:c0 + rows], moving,
                                         start=True, stop=True).then_inc(slot_full, 1)
                    elif kind == "DN":
                        c = stage[1]
                        rows = chunk_rows(c)
                        if c == 0:
                            pe.wait_ge(y_out.sem, y_out.at(i, 0))
                        pe.wait_ge(h_done.sem, h_done.at(i, c + 1))
                        last = nc.tensor.matmul(y_ps[:, 0:N], w_down[0:rows, c, :], hid[0:rows, c % R, :],
                                                start=(c == 0), stop=(c == C - 1 and n == 1))
                        last.then_inc(h_used.sem, 1)
                    elif kind == "M":
                        g, u = stage[1], stage[2]
                        if u == 0:
                            rows_in = stack_in[g].at if g else stack_in[g].next
                            pe.wait_ge(stack_in[g].sem, rows_in(i, 6 * 16))
                        h, j0 = g * HG + u // 2, 2 * (u % 2)
                        for a in range(2):
                            last = nc.tensor.matmul(ps[:, a * BANK:a * BANK + N],
                                                    q_stack[0:STACK, h, (j0 + a) * P:(j0 + a + 1) * P],
                                                    k_stack[0:STACK, h, :], start=True, stop=True)
                        last.then_inc(slot_full, 1)
                    elif kind == "NT":
                        g = stage[1]
                        pe.wait_ge(mxp_done.sem, mxp_done.at(i, g + 1))
                        psb = ps[:, 0:BANK].bitcast(BF16)
                        for j in range(J):
                            last = nc.tensor.transpose(psb[0:3 * HG, j * P:(j + 1) * P],
                                                       mx_parts[:, g, j].rearrange("p a h -> p (a h)"), ident_b[:])
                        last.then_inc(slot_full, 1)
                    elif kind == "E":
                        g, j, half = stage[1:]
                        if j == 0 and half == 0:
                            pe.wait_ge(mx_in[g].sem, mx_in[g].at(i, 16))
                        for a in range(2):
                            h = g * HG + 2 * half + a
                            last = nc.tensor.matmul(ps[:, a * BANK:a * BANK + N],
                                                    k_stack[0:STACK + MAXROWS, h, j * P:(j + 1) * P],
                                                    q_stack[:, h, :], start=True, stop=True)
                        last.then_inc(slot_full, 1)
                    elif kind == "PV":
                        g, j = stage[1:]
                        if (g, j) == (0, 0):
                            pe.wait_ge(hand_v_done.sem, hand_v_done.at(i, 1))
                        if j == 0:
                            pe.wait_ge(pv_out.sem, pv_out.at(i, g))
                        if not ph.same(("E", g, j, 0), ("E", g, j, 1)):
                            pe.wait_ge(emptied(ph, ("E", g, j, 0)), emptied_at(ph, i, ("E", g, j, 0)))
                        pe.wait_ge(emptied(ph, ("E", g, j, 1)), emptied_at(ph, i, ("E", g, j, 1)))
                        for a in range(HG):
                            last = nc.tensor.matmul(pv_ps[a * VW:(a + 1) * VW, 0:N], v[:, j, g * HG + a, :],
                                                    probsT[:, j, a, :], start=(j == 0), stop=(j == J - 1),
                                                    skip_group_check=True)
                        last.then_inc(p_used.sem, 1)
                    elif kind == "AT":
                        g = stage[1]
                        pe.wait_ge(pv_out.sem, pv_out.at(i, g + 1 - 0))
                        for j in range(J):
                            last = nc.tensor.transpose(ps[:, j * P:(j + 1) * P],
                                                       pv_sb[:, g % 2, j * P:(j + 1) * P], ident[:])
                        last.then_inc(slot_full, 1)
                    elif kind == "OT":
                        if not ph.same(stage, ("AT", G - 1)):
                            pe.wait_ge(emptied(ph, ("AT", G - 1)), emptied_at(ph, i, ("AT", G - 1)))
                        for j in range(J):
                            last = nc.tensor.transpose(ps[:, j * P:(j + 1) * P], att[:, j, :], ident[:])
                        last.then_inc(slot_full, 1)
                    elif kind == "OY":
                        pe.wait_ge(emptied(ph, ("OT",)), emptied_at(ph, i, ("OT",)))
                        nc.tensor.matmul(y_ps[:, 0:N], wo, attT[:], start=False, stop=True).then_inc(y_full.sem, 1)
                    elif kind == "YT":
                        pe.wait_ge(y_out.sem, y_out.at(i, 1))
                        for j in range(J):
                            last = nc.tensor.transpose(ps[:, j * P:(j + 1) * P], y_sb[:, j * P:(j + 1) * P], ident[:])
                        last.then_inc(slot_full, 1)

            turn(first, -1)
            pe.wait_ge(sel_set, 2)
            pe.wait_ge(loaded[2], 32)
            pe.wait_ge(loaded[3], 16 if n == 0 else 48)
            with pe.Fori(0, B - 1, 1) as i:
                turn(body, i)
            turn(last, B - 1)

        @block.scalar
        def _(sc):
            if n == 0:
                sc.wait_ge(loaded[0], 96)
            def turn(ph, i):
                for stage in ph.order:
                    kind = stage[0]
                    if stage in ph.ring:
                        ps = slot[ph.slot(stage)]
                        slot_free = emptied(ph, stage)
                    if kind == "XT":
                        sc.wait_ge(filled(ph, stage), filled_at(ph, i, stage))
                        nc.scalar.activation(xnT_next[:], ps[:, 0:N], ACT.Copy).then_inc(slot_free, 1)
                    elif kind == "QK":
                        sc.wait_ge(filled(ph, stage), filled_at(ph, i, stage))
                        if n == 0:
                            nc.scalar.activation(qk_raw[:, 0, :], ps[:, 0:N], ACT.Identity,
                                                 bias=cols[:, 0:1]).then_inc(qkraw_done.sem, 1)
                            nc.scalar.activation(qk_raw[:, 1, :], ps[:, BANK:BANK + N], ACT.Identity,
                                                 bias=cols[:, 1:2]).then_inc(slot_free, 1)
                        else:
                            nc.scalar.activation(qk[:], ps[:].rearrange("p (a t) -> p a t", a=2), ACT.Copy)\
                                .then_inc(slot_free, 1)
                    elif kind == "MS":
                        sc.wait_ge(filled(ph, stage), filled_at(ph, i, stage))
                        nc.scalar.activation(rinv[:].rearrange("p a t -> p (a t)"), ps[:], ACT.Sqrt, bias=cols[:, 5:6])\
                            .then_inc(slot_free, 1)
                    elif kind == "HI":
                        if n == 0:
                            sc.wait_ge(qk_done.sem, qk_done.next(i, 2))
                        else:
                            sc.wait_ge(emptied(ph, ("QK",)), emptied_at(ph, i, ("QK",)))
                        sc.wait_ge(parts_out.sem, parts_out.next(i, 0))
                        nc.scalar.activation(parts[:, :, 0], qk[:], ACT.Copy).then_inc(hi_done.sem, 1)
                    elif kind == "RT":
                        if n == 0:
                            sc.wait_ge(gate_raw.sem, gate_raw.next(i, 1))
                            nc.scalar.activation(gate[:], gate[:], ACT.Tanh, scale=0.5)\
                                .then_inc(gate_tanh.sem, 1)
                        sc.wait_ge(logits_done.sem, logits_done.next(i, 1))
                        nc.scalar.activation(probs[:, :, 0:E], logits[:], ACT.Exp).then_inc(exp_routed.sem, 1)
                    elif kind == "CW":
                        sc.wait_ge(filled(ph, stage), filled_at(ph, i, stage))
                        nc.scalar.activation(cwT[:], ps[:, 0:BANK].bitcast(BF16)[0:3 * E, 0:N], ACT.Copy)\
                            .then_inc(slot_free, 1)
                    elif kind == "GU":
                        c = stage[1]
                        rows = chunk_rows(c)
                        sc.wait_ge(filled(ph, stage), filled_at(ph, i, stage))
                        sc.wait_ge(h_done.sem, h_done.at(i, c + 1 - R))
                        nc.scalar.activation(up[0:rows, c % R, :], ps[0:rows, BANK:BANK + N], ACT.Copy, scale=0.5)\
                            .then_inc(actgu.sem, 1)
                        nc.scalar.activation(th[0:rows, c % R, :], ps[0:rows, 0:N], ACT.Tanh, scale=0.5)\
                            .then_inc(actgu.sem, 1)
                    elif kind == "NT":
                        g = stage[1]
                        sc.wait_ge(filled(ph, stage), filled_at(ph, i, stage))
                        nc.scalar.activation(mxT[:, g, :], ps[:, 0:BANK].bitcast(BF16)[0:3 * HG, 0:N], ACT.Copy)\
                            .then_inc(slot_free, 1)
                    elif kind == "E":
                        g, j, half = stage[1:]
                        sc.wait_ge(filled(ph, stage), filled_at(ph, i, stage))
                        if half == 0:
                            sc.wait_ge(p_used.sem, p_used.at(i, g * J + j + 1 - J))
                        nc.scalar.activation(probsT[:, j, 2 * half:2 * half + 2, :],
                                             ps[:].rearrange("p (a t) -> p a t", a=2), ACT.Exp, scale=SCALE)\
                            .then_inc(slot_free, 1)
                    elif kind == "PO":
                        g = stage[1]
                        sc.wait_ge(p_used.sem, p_used.at(i, (g + 1) * J))
                        nc.scalar.activation(pv_sb[:, g % 2, :], pv_ps[:], ACT.Copy).then_inc(pv_out.sem, 1)
                    elif kind == "OT":
                        sc.wait_ge(filled(ph, stage), filled_at(ph, i, stage))
                        nc.scalar.activation(attT[:], ps[:, 0:N], ACT.Copy).then_inc(slot_free, 1)
                    elif kind == "YT":
                        if n == 0:
                            sc.wait_ge(y_full.sem, y_full.at(i, 1))
                            nc.scalar.activation(y_sb[:], y_ps[:], ACT.Identity, bias=cols[:, 4:5])\
                                .then_inc(y_out.sem, 1)
                        else:
                            sc.wait_ge(h_used.sem, h_used.at(i, C))
                            nc.scalar.activation(y_sb[:], y_ps[:], ACT.Copy).then_inc(y_out.sem, 1)

            turn(first, -1)
            with sc.Fori(0, B - 1, 1) as i:
                turn(body, i)
            turn(last, B - 1)

        @block.vector
        def _(ve):
            used = [0]

            def link(ph, i, ins, alone=False):
                used[0] += 1
                ins.then_inc(dve_chain.sem, 1)
                ve.wait_ge(dve_chain.sem, ph.link(i, "dve", used[0]))
                if alone:
                    carry(ve)

            nc.vector.memset(minus_half[:], -0.5).then_inc(consts_set, 1)
            nc.vector.memset(v[:], 1.0).then_inc(consts_set, 1)
            nc.vector.memset(probs[:], NOT_THERE).then_inc(consts_set, 1)
            nc.vector.memset(top2[:], NOT_THERE).then_inc(consts_set, 1)
            ve.wait_ge(loaded[0], 96 if n == 0 else 32)
            nc.vector.tensor_copy(ident_b[:], ident[:]).then_inc(sel_set, 1)
            ve.wait_ge(consts_set, 4)
            def turn(ph, i):
                used[0] = 0
                for stage in ph.order:
                    kind = stage[0]
                    if stage in ph.ring:
                        ps = slot[ph.slot(stage)]
                        slot_free = emptied(ph, stage)
                    if kind == "LN":
                        for j in range(J):
                            last = nc.vector.bn_stats(stats[:, j, :], x_all[:, bass.ds(i * J + (J + j), 1), :].rearrange("p a d -> p (a d)"))
                        link(ph, i, last, alone=True)
                        for j in range(J):
                            last = nc.vector.bn_aggr(mv[:, j, :], stats[:, j, :])
                        link(ph, i, last)
                        nc.vector.tensor_scalar(var_eps[:], mv[:, :, 1], LN_EPS, None, ALU.add).then_inc(var_done.sem, 1)
                    elif kind == "XN":
                        ve.wait_ge(rstd_done.sem, rstd_done.next(i, 1))
                        for j in range(J):
                            last = nc.vector.tensor_scalar(xn[:, j, :], x_all[:, bass.ds(i * J + (J + j), 1), :].rearrange("p a d -> p (a d)"),
                                                           mv[:, j, 0:1], rstd[:, j:j + 1], ALU.subtract, ALU.mult)
                        last.then_inc(ln_done.sem, 1)
                    elif kind == "VG":
                        ve.wait_ge(filled(ph, stage), filled_at(ph, i, stage))
                        both = ps[:].rearrange("p (a t) -> p a t", a=2)[:, :, 0:2 * VGW].rearrange("p a (b w) -> p a b w", b=2)
                        v4 = v_next[:].rearrange("p (a b) d -> p a b d", a=2)
                        if n == 0:
                            bv = bias_vg[:, 0:D].unsqueeze(1).unsqueeze(1).broadcast_to([P, 2, 2, D])
                            nc.vector.tensor_tensor(v4, both[:, :, :, 0:D], bv, ALU.add)
                            bg = bias_vg[:, D:D + H].unsqueeze(1).unsqueeze(1).broadcast_to([P, 2, 2, H])
                            nc.vector.tensor_tensor(gate[:].rearrange("p (a b) e -> p a b e", a=2), both[:, :, :, D:D + H],
                                                    bg, ALU.add).then_inc(gate_raw.sem, 1)
                        else:
                            nc.vector.tensor_copy(v4, both[:, :, :, 0:D])
                        nc.vector.tensor_copy(logits[:].rearrange("p (a b) e -> p a b e", a=2), both[:, :, :, VGW - E:VGW])\
                            .then_inc(slot_free, 1)
                    elif kind == "RC":
                        k = stage[1]
                        if k == 0:
                            ve.wait_ge(emptied(ph, ("MS",)), emptied_at(ph, i, ("MS",)))
                        quarter = rinv[:].rearrange("p a t -> p (a t)")[:, k * 256:(k + 1) * 256]
                        nc.vector.reciprocal(quarter, quarter).then_inc(rc_done.sem, 1)
                    elif kind == "QN":
                        ve.wait_ge(rc_done.sem, rc_done.next(i, 4))
                        for a in range(2):
                            nc.vector.scalar_tensor_tensor(out=qk[:, a, :], in0=qk_raw[:, a, :], scalar=cols[:, 2 + a:3 + a],
                                                           in1=rinv[:, a, :], op0=ALU.mult, op1=ALU.mult)\
                                .then_inc(qk_done.sem, 1)
                    elif kind == "HAND":
                        nc.vector.tensor_copy(xnT[:], xnT_next[:]).then_inc(hand_done.sem, 1)
                        ve.wait_ge(p_used.sem, p_used.next(i, 0))
                        ve.wait_ge(emptied(ph, ("VG",)), emptied_at(ph, i, ("VG",)))
                        nc.vector.tensor_copy(v[:, :, :, 0:HD], v_next[:].rearrange("p j (h d) -> p j h d", h=H))\
                            .then_inc(hand_v_done.sem, 1)
                        if n == 0:
                            ve.wait_ge(gate_tanh.sem, gate_tanh.next(i, 1))
                            link(ph, i, nc.vector.tensor_scalar(gate_sig[:], gate[:], 1.0, 0.5, ALU.add, ALU.mult))
                    elif kind == "RT":
                        ve.wait_ge(emptied(ph, ("VG",)), emptied_at(ph, i, ("VG",)))
                        link(ph, i, nc.vector.tensor_reduce(lmax[:], logits[:], AXIS.X, ALU.max))
                        nc.vector.tensor_tensor(logits[:], logits[:], lmax[:].unsqueeze(2).broadcast_to([P, J, E]),
                                                ALU.subtract).then_inc(logits_done.sem, 1)
                    elif kind == "RW":
                        p = probs[:, :, 0:E]
                        ve.wait_ge(exp_routed.sem, exp_routed.next(i, 1))
                        link(ph, i, nc.vector.tensor_reduce(psum_[:], p, AXIS.X, ALU.add))
                        link(ph, i, nc.vector.reciprocal(psum_[:], psum_[:]))
                        link(ph, i, nc.vector.tensor_tensor(p, p, psum_[:].unsqueeze(2).broadcast_to([P, J, E]), ALU.mult),
                             alone=True)
                        for j in range(J):
                            last = nc.vector.max(top8[:, j, :], probs[:, j, 0:E])
                        link(ph, i, last)
                        link(ph, i, nc.vector.tensor_copy(top2[:, :, 0:2], top8[:, :, 0:2]), alone=True)
                        for j in range(J):
                            last = nc.vector.match_replace(marked[:, j, :], top2[:, j, :], probs[:, j, :], TAKEN)
                        link(ph, i, last)
                        c_in = nc.vector.scalar_tensor_tensor(out=cw[:], in0=marked[:, :, 0:E], scalar=(NOT_THERE + TAKEN) / 2,
                                                              in1=p, op0=ALU.is_lt, op1=ALU.mult)
                        if n == 0:
                            c_in.then_inc(cw_done.sem, 1)
                        else:
                            link(ph, i, c_in)
                            link(ph, i, nc.vector.tensor_tensor(psum_[:], top8[:, :, 0], top8[:, :, 1], ALU.add))
                            link(ph, i, nc.vector.tensor_scalar(psum_[:], psum_[:], 1e-20, None, ALU.add))
                            link(ph, i, nc.vector.reciprocal(psum_[:], psum_[:]))
                            nc.vector.tensor_tensor(cw[:], cw[:], psum_[:].unsqueeze(2).broadcast_to([P, J, E]), ALU.mult)\
                                .then_inc(cw_done.sem, 1)
                    elif kind == "BC":
                        e = stage[1]
                        ve.wait_ge(filled(ph, stage), filled_at(ph, i, stage))
                        if n == 1:
                            if e == 0:
                                ve.wait_ge(hand_done.sem, hand_done.at(i, 1))
                            nc.vector.tensor_tensor(xe[:, e % 2, :], xnT[:], ps[:, 0:N], ALU.mult).then_inc(slot_free, 1)
                        else:
                            c = e + 1
                            ve.wait_ge(h_done.sem, h_done.at(i, c + 1 - R))
                            nc.vector.tensor_tensor(upc[:, c % R, :], up[:, c % R, :], ps[:, 0:N], ALU.mult)\
                                .then_inc(slot_free, 1)
                    elif kind == "GA":
                        c = stage[1]
                        rows = chunk_rows(c)
                        ps = slot[ph.slot(("GU", c))]
                        ve.wait_ge(actgu.sem, actgu.at(i, 2 * (c + 1)))
                        ve.wait_ge(h_done.sem, h_done.at(i, c + 1 - R))
                        ve.wait_ge(filled(ph, ("GU", c)), filled_at(ph, i, ("GU", c)))
                        nc.vector.scalar_tensor_tensor(out=act[0:rows, c % R, :], in0=th[0:rows, c % R, :], scalar=1.0,
                                                       in1=ps[0:rows, 0:N], op0=ALU.add, op1=ALU.mult)\
                            .then_inc(emptied(ph, ("GU", c)), 1)
                    elif kind == "M":
                        g, u = stage[1], stage[2]
                        hh, j0 = u // 2, 2 * (u % 2)
                        ve.wait_ge(filled(ph, stage), filled_at(ph, i, stage))
                        nc.vector.tensor_reduce(mx[:, g, hh, j0:j0 + 2], ps[:].rearrange("p (a t) -> p a t", a=2),
                                                AXIS.X, ALU.max).then_inc(slot_free, 1)
                    elif kind == "AT":
                        g = stage[1]
                        ve.wait_ge(filled(ph, stage), filled_at(ph, i, stage))
                        src = ps[:, 0:N].rearrange("p (j h c) -> p j h c", j=J, h=HG)
                        link(ph, i, nc.vector.reciprocal(inv[:], src[:, :, :, HD]))
                        use = inv
                        if n == 0:
                            link(ph, i, nc.vector.tensor_tensor(inv2[:], inv[:], gate_sig[:, :, g * HG:(g + 1) * HG], ALU.mult))
                            use = inv2
                        dst = att[:, :, g * HG * HD:(g + 1) * HG * HD].rearrange("p j (h d) -> p j h d", h=HG)
                        nc.vector.tensor_tensor(dst, src[:, :, :, 0:HD], use[:].unsqueeze(3).broadcast_to([P, J, HG, HD]),
                                                ALU.mult).then_inc(slot_free, 1)
                    elif kind == "YT":
                        ve.wait_ge(filled(ph, stage), filled_at(ph, i, stage))
                        xs = x_all[:, bass.ds(i * J, J), :]
                        y = ps[:, 0:N].rearrange("p (j d) -> p j d", j=J)
                        if n == 0:
                            nc.vector.tensor_tensor(xs, xs, y, ALU.add).then_inc(slot_free, 1)
                        else:
                            ve.wait_ge(out_dma.sem, out_dma.at(i, 0))
                            nc.vector.tensor_tensor(out_sb[:], xs, y, ALU.add).then_inc(slot_free, 1)
                            ve.wait_ge(emptied(ph, stage), emptied_at(ph, i, stage))
                            nc.vector.tensor_tensor(out_sb[:], out_sb[:], att[:], ALU.add).then_inc(out_done.sem, 1)
                assert used[0] == ph.links["dve"], (n, ph.main, ph.setup, used, ph.links)

            turn(first, -1)
            ve.wait_ge(loaded[1], 16)
            nc.vector.tensor_copy(select[:], select_f[:]).then_inc(sel_set, 1)
            with ve.Fori(0, B - 1, 1) as i:
                turn(body, i)
            turn(last, B - 1)

        @block.gpsimd
        def _(gp):
            used = [0]

            def link(ph, i, ins):
                used[0] += 1
                ins.then_inc(pool_chain.sem, 1)
                gp.wait_ge(pool_chain.sem, ph.link(i, "pool", used[0]))
                carry(gp)

            nc.gpsimd.memset(k_stack[64:96].rearrange("p h t -> p (h t)").bitcast(F32), TWO_ONES).then_inc(ones_set, 1)
            for t in (*free, parts_out, h_done, h_used, p_used, pv_out, y_out, out_dma):
                gp.sem_inc(t.sem, t.credit)
            gp.wait_ge(consts_set, 4)
            gp.wait_ge(ones_set, 1)
            def turn(ph, i):
                used[0] = 0
                for stage in ph.order:
                    kind = stage[0]
                    if kind == "LN":
                        gp.wait_ge(var_done.sem, var_done.next(i, 1))
                        nc.gpsimd.tensor_tensor(rstd[:], var_eps[:], minus_half[:].broadcast_to([P, J]), ALU.pow)\
                            .then_inc(rstd_done.sem, 1)
                    elif kind == "SQ":
                        gp.wait_ge(qkraw_done.sem, qkraw_done.next(i, 1))
                        gp.wait_ge(emptied(ph, ("QK",)), emptied_at(ph, i, ("QK",)))
                        nc.gpsimd.tensor_tensor(squares[:], qk_raw[:], qk_raw[:], ALU.mult).then_inc(sq_done.sem, 1)
                    elif kind == "PT":
                        gp.wait_ge(hi_done.sem, hi_done.next(i, 1))
                        link(ph, i, nc.gpsimd.tensor_tensor(rest[:], qk[:], parts[:, :, 0], ALU.subtract))
                        link(ph, i, nc.gpsimd.tensor_tensor(parts[:, :, 1], qk[:], parts[:, :, 0], ALU.subtract))
                        nc.gpsimd.tensor_tensor(parts[:, :, 2], rest[:], parts[:, :, 1], ALU.subtract)\
                            .then_inc(parts_done.sem, 1)
                    elif kind == "RW":
                        gp.wait_ge(cw_done.sem, cw_done.next(i, 1))
                        carry(gp)
                        link(ph, i, nc.gpsimd.tensor_copy(cw_parts[:, :, 0, :], cw[:]))
                        link(ph, i, nc.gpsimd.tensor_tensor(cw_rest[:], cw[:], cw_parts[:, :, 0, :], ALU.subtract))
                        link(ph, i, nc.gpsimd.tensor_copy(cw_parts[:, :, 1, :], cw_rest[:]))
                        nc.gpsimd.tensor_tensor(cw_parts[:, :, 2, :], cw_rest[:], cw_parts[:, :, 1, :], ALU.subtract)\
                            .then_inc(cwp_done.sem, 1)
                    elif kind == "GA":
                        c = stage[1]
                        rows = chunk_rows(c)
                        if n == 1 or c == 0:
                            gp.wait_ge(emptied(ph, ("GU", c)), emptied_at(ph, i, ("GU", c)))
                            gp.wait_ge(h_used.sem, h_used.at(i, c + 1 - R))
                            nc.gpsimd.tensor_tensor(hid[0:rows, c % R, :], act[0:rows, c % R, :], up[0:rows, c % R, :],
                                                    ALU.mult).then_inc(h_done.sem, 1)
                    elif kind == "BC" and n == 0:
                        c = stage[1] + 1
                        gp.wait_ge(emptied(ph, ("GU", c)), emptied_at(ph, i, ("GU", c)))
                        gp.wait_ge(emptied(ph, stage), emptied_at(ph, i, stage))
                        gp.wait_ge(h_used.sem, h_used.at(i, c + 1 - R))
                        nc.gpsimd.tensor_tensor(hid[:, c % R, :], act[:, c % R, :], upc[:, c % R, :],
                                                ALU.mult).then_inc(h_done.sem, 1)
                    elif kind == "M" and stage[2] == 7:
                        g = stage[1]
                        for u in range(8):
                            if all(ph.slot(("M", g, w)) != ph.slot(("M", g, u)) for w in range(u + 1, 8)):
                                gp.wait_ge(emptied(ph, ("M", g, u)), emptied_at(ph, i, ("M", g, u)))
                        carry(gp)
                        hi, mid, lo = (mx_parts[:, g, :, a, :] for a in range(3))
                        link(ph, i, nc.gpsimd.tensor_scalar(mx_neg[:], mx[:, g].rearrange("p h j -> p j h"), -1.0, None, ALU.mult))
                        link(ph, i, nc.gpsimd.tensor_copy(hi, mx_neg[:]))
                        link(ph, i, nc.gpsimd.tensor_tensor(mx_rest[:], mx_neg[:], hi, ALU.subtract))
                        link(ph, i, nc.gpsimd.tensor_copy(mid, mx_rest[:]))
                        nc.gpsimd.tensor_tensor(lo, mx_rest[:], mid, ALU.subtract).then_inc(mxp_done.sem, 1)
                assert used[0] == ph.links["pool"], (n, ph.main, ph.setup, used, ph.links)

            turn(first, -1)
            with gp.Fori(0, B - 1, 1) as i:
                turn(body, i)
            turn(last, B - 1)


def layers():
    return (
        {"n": 0, "E": 16, "chunks": 9, "hidden": 9 * P, "vgw": D + H + 16, "att_cols": 2 * D + (D + H + 16) + D,
         "span": 4.2, "lag": 1.5, "values": 3.6, "gate": 0.03,
         "links": {"dve": (10, 8), "pool": (9, 12)}},
        {"n": 1, "E": 8, "chunks": 24, "hidden": 8 * 352, "vgw": D + 8, "att_cols": 2 * D + (D + 8),
         "span": 4.4, "lag": 2.5, "values": 3.6, "gate": 0.03,
         "links": {"dve": (13, 4), "pool": (9, 12)}},
    )


def two_layers(nc, h0, h1):
    with ExitStack() as ctx:
        x_all = ctx.enter_context(nc.sbuf_tensor("x_all", [P, B * J, D], F32))
        l0, l1 = layers()
        layer_block(nc, l0, x_all, h0)
        layer_block(nc, l1, x_all, h1)


def kernel(**inputs):
    import numpy as np
    import concourse.bacc as bacc
    from concourse.bass_utils import run_bass_kernel_spmd

    x = {k: np.asarray(a) for k, a in inputs.items()}
    by_d = np.arange(D).reshape(H, HD).T.reshape(D)
    per_d = np.repeat(np.arange(HD), H)
    f0, f1 = x["L0_ffn_Wg"], x["L1_ffn_W1"]

    def side(a):
        return np.transpose(a, (1, 0, 2)).reshape(D, -1)

    wq0 = x["L0_attn_Wq"]
    eye = np.eye(P, dtype=np.float32)
    sel0 = np.zeros((3, 16, 8, P), np.float32)
    sel1 = np.zeros((3, 8, 8, P), np.float32)
    for c in range(8):
        sel0[:, 2 * c, c, 0:64] = 1.0
        sel0[:, 2 * c + 1, c, 64:128] = 1.0
        sel1[:, c, c, :] = 1.0
    head_mean = (np.arange(P)[:, None] % H == np.arange(P)[None] % H).astype(np.float32) / HD
    arrays0 = {
        "x": x["L0_attn_x"].reshape(B * N, D),
        "ident": eye,
        "select": sel0.reshape(48, 8 * P),
        "head_mean": head_mean,
        "cols": np.stack([x["L0_attn_bq"][:D][by_d], x["L0_attn_bk"][by_d], x["L0_attn_qn_w"][per_d],
                          x["L0_attn_kn_w"][per_d], x["L0_attn_bo"], np.full(D, RMS_EPS, np.float32)], axis=1),
        "bias_vg": np.concatenate([x["L0_attn_bv"], x["L0_attn_bq"][D:]]),
        "att": np.concatenate([wq0[:, :D][:, by_d], x["L0_attn_Wk"][:, by_d], x["L0_attn_Wv"], wq0[:, D:],
                               x["L0_ffn_Wr"], x["L0_attn_Wo"]], axis=1),
        "gate": np.concatenate([x["L0_ffn_Sg"], side(x["L0_ffn_Wg"])], axis=1),
        "up": np.concatenate([x["L0_ffn_Su"], side(x["L0_ffn_Wu"])], axis=1),
        "down": np.concatenate([x["L0_ffn_Sd"][None], x["L0_ffn_Wd"].reshape(8, P, D)]).transpose(1, 0, 2),
    }
    arrays1 = {
        "ident": eye,
        "select": sel1.reshape(24, 8 * P),
        "att": np.concatenate([x["L1_attn_Wq"].T[:, by_d], x["L1_attn_Wk"].T[:, by_d], x["L1_attn_Wv"].T,
                               x["L1_ffn_Wg"].T], axis=1),
        "gate": side(np.transpose(x["L1_ffn_W1"], (0, 2, 1))),
        "up": side(np.transpose(x["L1_ffn_W3"], (0, 2, 1))),
        "down": np.transpose(x["L1_ffn_W2"], (0, 2, 1)),
    }
    nc = bacc.Bacc("TRN2", target_bir_lowering=False, num_devices=1)
    given, hbm = {}, []
    for n, arrays in enumerate((arrays0, arrays1)):
        aps = {}
        for name, a in arrays.items():
            a = np.ascontiguousarray(a)
            full = f"in{n}_{name}"
            given[full] = a
            aps[name] = nc.dram_tensor(full, a.shape, mybir.dt.from_np(a.dtype), kind="ExternalInput").ap()
        aps["parts"] = nc.dram_tensor(f"parts{n}", (B, 2, 3, P, N), BF16, kind="Internal").ap()
        aps["maxima"] = nc.dram_tensor(f"maxima{n}", (B, G, 3 * HG, N), BF16, kind="Internal").ap()
        hbm.append(aps)
    hbm[1]["out"] = nc.dram_tensor("out", (B, N, D), F32, kind="ExternalOutput").ap()
    two_layers(nc, hbm[0], hbm[1])
    r = run_bass_kernel_spmd(nc, [given], core_ids=[0])
    return r.results[0]["out"]
```

```python
import concourse.bass as bass
from concourse import mybir
from contextlib import ExitStack
import struct

F32 = mybir.dt.float32
BF16 = mybir.dt.bfloat16
ACT = mybir.ActivationFunctionType
ALU = mybir.AluOpType
AXIS = mybir.AxisListType

B, N, D = 4, 512, 128
H, HD = 16, 8
P = 128
J = N // P
G, HG = 4, 4
VW = 32
STACK = 9 * HD
MAXROWS = 3
SLOTS = 6
BANK = 512
R = 3
AHEAD = 3
LN_EPS = 1e-5
RMS_EPS = 1e-6
SCALE = float(HD) ** -0.5
TWO_ONES = struct.unpack("<f", b"\x80\x3f\x80\x3f")[0]
NOT_THERE = -1.0
TAKEN = -2.0


class Tally:

    def __init__(self, nc, ctx, name, per, credit=0):
        self.sem = ctx.enter_context(nc.semaphore(name))
        self.per, self.credit = per, credit

    def at(self, i, k):
        return i * self.per + (self.credit + k)

    def of(self, i, c, k):
        return self.next(i, k) if c < AHEAD else self.at(i, k)

    def next(self, i, k):
        return i * self.per + (self.per + self.credit + k)


def stages(layer, main, setup):
    C, T = layer["chunks"], layer["times"]
    at = []

    def put(time, *found):
        at.append((time, len(at), found))

    def put_chunk(time, c):
        if layer["n"] == 1 and c in (0, AHEAD):
            put(time - 0.01, ("BC", c // 3))
        put(time, ("GG", c))
        put(time + T["up"], ("UU", c))
        put(time + T["up"] + T["gated"], ("GA", c))
        if layer["n"] == 1 and c >= AHEAD and c % 3 == 0 and c // 3 + 1 < layer["E"]:
            put(time + T["weights"], ("BC", c // 3 + 1))
        if layer["n"] == 0 and c >= 1:
            put(time + T["up"] + T["gated"] + T["weights"], ("BC", c - 1))

    step = T["span"] / (C - AHEAD)
    attended = G - 1 + T["sums"] + T["normalise"]
    expert_done = T["chunks"] + step * (C - AHEAD - 1) + T["up"] + T["gated"] + T["weights"]
    if main:
        for g in range(G):
            if g >= 1:
                for u in range(HG * J):
                    put(g - 1 + T["max"] + T["max_span"] * u / (HG * J), ("M", g, u))
            put(g + T["max_parts"], ("NT", g))
            for j in range(J):
                for a in range(HG):
                    put(g + T["exp"] + T["exp_span"] * (HG * j + a) / (HG * J), ("E", g, j, a))
                put(g + T["exp"] + T["exp_span"] * (j + T["exp_lead"]) / J, ("PV", g, j))
            put(g + T["sums"], ("PO", g))
            put(g + T["sums"] + T["normalise"], ("AT", g))
        for c in range(C):
            time = T["chunks"] + step * (c - AHEAD)
            if c >= AHEAD:
                put_chunk(time, c)
            put(min(max(time + T["lag"] * step, T["down"] + T["down_step"] * c), T["chunks"] + T["span"] + 0.001 * c), ("DN", c))
        if layer["n"] == 0:
            put(max(T["out"], attended + 0.001), ("OT",))
            put(max(T["out"], attended + 0.001) + T["out_lag"], ("OY",))
        put(max(T["result"], attended + 0.002), ("YT",))
    if setup:
        put(T["norm"], ("LN",))
        put(T["norm"] + 0.15, ("XN",))
        put(T["qk"] - 0.1, ("XT",))
        put(T["qk"], ("QK", 0))
        put(T["qk"], ("QK", 1))
        if layer["n"] == 0:
            put(T["qk"] + 0.05, ("SQ", 0))
            put(T["qk"] + 0.05, ("SQ", 1))
            put(T["squares"], ("MS", 0))
            put(T["squares"], ("MS", 1))
            for k in range(4):
                put(T["roots"] + T["roots_step"] * k, ("RC", k))
        for a in range(2):
            if layer["n"] == 0:
                put(T["roots"] + T["roots_step"] * (2 * a + 1) + 0.1, ("QN", a))
            cut = T["roots"] + T["roots_step"] * (2 * a + 1) + 0.15
            put(cut, ("HI", a))
            put(cut + 0.1, ("PT", a))
        put(2.2, ("RF", 0))
        put(2.4, ("RF", 1))
        put(3.3, ("RF", 2))
        put(4.3, ("RF", 3))
        for u in range(HG * J):
            put(3 + T["max"] + T["max_span"] * u / (HG * J), ("M", 0, u))
        values = T["values"] if main else T["first_values"]
        put(values, ("VG", 0))
        put(values, ("VG", 1))
        put(values + 0.05, ("RT",))
        put(values + T["route"], ("RW",))
        hand = max(T["hand"], attended + 0.003, expert_done + 0.002) if main else T["first_hand"]
        put(hand, ("HAND",))
        put(hand + T["ahead"], ("CW",))
        for c in range(AHEAD):
            put_chunk(hand + T["ahead"] + 0.02 + (T["ahead_step"] if main else T["first_step"]) * c, c)
    return [stage for _, _, found in sorted(at) for stage in found]


class Phase:

    def __init__(self, layer, main, setup, before=None):
        self.main, self.setup = main, setup
        self.order = stages(layer, main, setup)
        self.uses = [0] * SLOTS
        self.ring, self.nth = {}, {}
        for stage in self.order:
            if stage[0] in FILLS:
                s = len(self.ring) % SLOTS
                self.ring[stage] = s
                self.nth[stage] = self.uses[s]
                self.uses[s] += 1
        self.base = [0] * SLOTS
        self.per = [0] * SLOTS
        self.links = {e: layer["links"][e][0] * setup + layer["links"][e][1] * main for e in ("dve", "pool")}
        self.link_base = {"dve": 0, "pool": 0}
        self.link_per = {"dve": 0, "pool": 0}

    def follow(self, first, turn):
        self.base, self.per = first.uses, turn.uses
        self.link_base, self.link_per = first.links, turn.links
        return self

    def slot(self, stage):
        return self.ring[stage]

    def same(self, a, b):
        return self.slot(a) == self.slot(b)

    def last_of(self, found):
        return [a for k, a in enumerate(found) if all(not self.same(a, b) for b in found[k + 1:])]

    def count(self, i, stage):
        s = self.slot(stage)
        return i * self.per[s] + (self.base[s] + self.nth[stage]) if self.per[s] else self.nth[stage]

    def link(self, i, engine, k):
        return i * self.link_per[engine] + (self.link_base[engine] + k) if self.link_per[engine] else k


FILLS = {"XT", "QK", "VG", "MS", "CW", "BC", "GG", "UU", "M", "NT", "E", "AT", "OT", "YT"}


def layer_block(nc, layer, shared, hbm):
    n, E, C = layer["n"], layer["E"], layer["chunks"]
    VGW = layer["vgw"]
    first = Phase(layer, False, True)
    body = Phase(layer, True, True)
    body.follow(first, body)
    last = Phase(layer, True, False).follow(first, body)

    with ExitStack() as ctx:
        def sb(name, shape, dt=F32):
            return ctx.enter_context(nc.sbuf_tensor(f"{name}_{n}", shape, dt))

        x_all, ident, ident_b, k_stack, v, minus_half, top2, w_atts = shared
        w_att = w_atts[n]
        w_gate = sb("w_gate", [P, layer["hidden"]])
        w_up = sb("w_up", [P, layer["hidden"]])
        w_down = sb("w_down", [P, C, D])
        wq, wk = w_att[:, 0:D], w_att[:, D:2 * D]
        wvg = w_att[:, 2 * D:2 * D + VGW]
        select = sb("select", [3 * E, 8 * P], BF16)
        select_f = sb("select_f", [3 * E, 8 * P])
        if n == 0:
            wo = w_att[:, 2 * D + VGW:3 * D + VGW]
            cols = sb("cols", [P, 6])
            bias_vg = sb("bias_vg", [P, D + H])
            head_mean = sb("head_mean", [P, P])
            squares = sb("squares", [P, 2, N])
            rinv = sb("rinv", [P, 2, N])
            qk_raw = sb("qk_raw", [P, 2, N])
            gate = sb("gate", [P, J, H])
            gate_sig = sb("gate_sig", [P, J, H])
            attT = sb("attT", [P, N])
            upc = sb("upc", [P, R, N])
            rest = squares
        else:
            rest = sb("rest", [P, 2, N])
            xe = sb("xe", [P, 2, N])
            out_sb = sb("out_sb", [P, J, D])
        stats = sb("stats", [P, J, 6])
        mv = sb("mv", [P, J, 2])
        rstd = sb("rstd", [P, J])
        var_eps = sb("var_eps", [P, J])
        xn = sb("xn", [P, J, D])
        xnT = sb("xnT", [P, N])
        qk = sb("qk", [P, 2, N])
        parts = sb("parts", [P, 2, 3, N], BF16)
        q_stack = sb("q_stack", [STACK + MAXROWS, H, N], BF16)
        v_next = sb("v_next", [P, J, D])
        xnT_next = sb("xnT_next", [P, N])
        logits = sb("logits", [P, J, E])
        lmax = sb("lmax", [P, J])
        probs = sb("probs", [P, J, E + 6])
        psum_ = sb("prob_sum", [P, J])
        top8 = sb("top8", [P, J, 8])
        marked = sb("marked", [P, J, E + 6])
        cw = sb("cw", [P, J, E])
        cw_rest = sb("cw_rest", [P, J, E])
        cw_parts = sb("cw_parts", [P, J, 3, E], BF16)
        cwT = sb("cwT", [3 * E, N], BF16)
        mx = sb("mx", [P, G, HG, J])
        mx_neg = sb("mx_neg", [P, J, HG])
        mx_rest = sb("mx_rest", [P, J, HG])
        mx_parts = sb("mx_parts", [P, G, J, 3, HG], BF16)
        mxT = sb("mxT", [3 * HG, G, N], BF16)
        probsT = sb("probsT", [P, J, HG, N])
        pv_sb = sb("pv_sb", [P, 2, N])
        inv = sb("inv", [P, J, HG])
        inv2 = sb("inv2", [P, J, HG])
        att = sb("att", [P, J, D])
        th = sb("th", [P, R, N])
        up = sb("up", [P, R, N])
        act = sb("act", [P, R, N])
        hid = sb("hid", [P, R, N])
        y_sb = sb("y_sb", [P, N])

        slot = [ctx.enter_context(nc.psum_tensor(f"slot{s}_{n}", [P, BANK], F32)) for s in range(SLOTS)]
        pv_ps = ctx.enter_context(nc.psum_tensor(f"pv_ps_{n}", [P, BANK], F32))
        y_ps = ctx.enter_context(nc.psum_tensor(f"y_ps_{n}", [P, BANK], F32))

        def tally(name, per, credit=0):
            return Tally(nc, ctx, f"{name}_{n}", per, credit)

        full = [tally(f"full{s}", 0) for s in range(SLOTS)]
        free = [tally(f"free{s}", 0, 1) for s in range(SLOTS)]
        loaded = [ctx.enter_context(nc.semaphore(f"loaded{k}_{n}")) for k in range(4)]
        consts_set = ctx.enter_context(nc.semaphore(f"consts_set_{n}"))
        x_in = ctx.enter_context(nc.semaphore(f"x_in_{n}"))
        ones_set = ctx.enter_context(nc.semaphore(f"ones_set_{n}"))
        sel_set = ctx.enter_context(nc.semaphore(f"sel_set_{n}"))
        carried = ctx.enter_context(nc.semaphore(f"carried_{n}"))
        ln_done = tally("ln_done", 1)
        var_done = tally("var_done", 1)
        rstd_done = tally("rstd_done", 1)
        sq_done = tally("sq_done", 2)
        qk_done = tally("qk_done", 2)
        hi_done = tally("hi_done", 2)
        parts_done = tally("parts_done", 2)
        parts_out = [tally(f"{a}_parts_out", 16, 16) for a in "qk"]
        stack_in = [tally(f"stack_in{g}", 6 * 16) for g in range(G)]
        hand_done = tally("hand_done", 1)
        hand_v_done = tally("hand_v_done", 1)
        rc_done = tally("rc_done", 4)
        logits_done = tally("logits_done", 1)
        gate_raw = tally("gate_raw", 2)
        gate_tanh = tally("gate_tanh", 1)
        exp_routed = tally("exp_routed", 1)
        cw_done = tally("cw_done", 1)
        cwp_done = tally("cwp_done", 1)
        th_done = tally("th_done", C)
        h_done = tally("h_done", C, R)
        h_used = tally("h_used", C, R)
        mxp_done = tally("mxp_done", G)
        mx_out = [tally(f"mx_out{g}", 16) for g in range(G)]
        mx_in = [tally(f"mx_in{g}", 16) for g in range(G)]
        p_used = tally("p_used", G * J, J)
        pv_full = tally("pv_full", G)
        pv_out = tally("pv_out", G, 1)
        y_full = tally("y_full", 1)
        y_out = tally("y_out", 1, 1)
        out_done = tally("out_done", 1)
        out_dma = tally("out_dma", 16, 16)
        dve_chain = tally("dve_chain", 0)
        pool_chain = tally("pool_chain", 0)

        def chunk_rows(c):
            return 96 if n == 1 and c % 3 == 2 else P

        def chunk_col(c):
            return (c // 3) * 352 + (c % 3) * P if n == 1 else c * P

        def filled(ph, stage):
            return full[ph.slot(stage)].sem

        def filled_at(ph, i, stage):
            return ph.count(i, stage) + 1

        def emptied(ph, stage):
            return free[ph.slot(stage)].sem

        def emptied_at(ph, i, stage):
            return ph.count(i, stage) + 2

        def vacant_at(ph, i, stage):
            return ph.count(i, stage) + 1

        def carry(eng):
            eng.sem_inc(carried, 1)

        block = ctx.enter_context(nc.Block())

        @block.sync
        def _(sp):
            if n == 0:
                x_tiles = hbm["x"].rearrange("(t p) d -> p t d", p=P)
                sp.dma_start(x_all[:, 0:J], x_tiles[:, 0:J]).then_inc(x_in, 16)
                sp.dma_start(ident[:], hbm["ident"]).then_inc(loaded[0], 16)
                sp.dma_start(w_att[:], hbm["att"]).then_inc(loaded[0], 16)
                sp.dma_start(cols[:], hbm["cols"]).then_inc(loaded[0], 16)
                sp.dma_start(head_mean[:], hbm["head_mean"]).then_inc(loaded[0], 16)
                sp.dma_start(bias_vg[:], hbm["bias_vg"].partition_broadcast(P)).then_inc(loaded[0], 16)
                sp.dma_start(x_all[:, J:B * J], x_tiles[:, J:B * J]).then_inc(loaded[1], 16)
            sp.dma_start(select_f[:], hbm["select"]).then_inc(loaded[1], 16)
            sp.dma_start(w_gate[:], hbm["gate"]).then_inc(loaded[2], 16)
            sp.dma_start(w_up[:], hbm["up"]).then_inc(loaded[2], 16)
            if n == 0:
                sp.dma_start(w_down[:], hbm["down"]).then_inc(loaded[3], 16)
                sp.dma_start(w_atts[1][:], hbm["next_att"]).then_inc(loaded[3], 16)
            else:
                for part in range(3):
                    rows = min(P, 352 - part * P)
                    sp.dma_start(w_down[0:rows, part:C:3, :],
                                 hbm["down"][:, part * P:part * P + rows, :].rearrange("e f d -> f e d"))\
                      .then_inc(loaded[3], 16)
            if n == 0:
                sp.wait_ge(ones_set, 1)
            def turn(ph, i):
                for stage in ph.order:
                    kind = stage[0]
                    if kind == "RF":
                        g = stage[1]
                        if g == 0:
                            for a in range(2):
                                sp.wait_ge(parts_done.sem, parts_done.next(i, a + 1))
                                carry(sp)
                                sp.dma_start(hbm["parts"][i + 1, a].rearrange("k p t -> p k t"), parts[:, a])\
                                  .then_inc(parts_out[a].sem, 16)
                        if ph.main:
                            sp.wait_ge(p_used.sem, p_used.at(i, (g + 1) * J))
                            carry(sp)
                        heads = slice(g * HG, (g + 1) * HG)
                        q_rows = hbm["parts"][i + 1, 0].rearrange("k (d h) t -> (k d) h t", h=H)[:, heads, :]
                        if g == 0:
                            sp.wait_ge(parts_out[0].sem, parts_out[0].next(i, 16))
                            carry(sp)
                        for b in range(3):
                            sp.dma_start(q_stack[b * 3 * HD:(b + 1) * 3 * HD, heads, :], q_rows)\
                              .then_inc(stack_in[g].sem, 16)
                        if g == 0:
                            sp.wait_ge(parts_out[1].sem, parts_out[1].next(i, 16))
                            carry(sp)
                        for b in range(3):
                            k_rows = hbm["parts"][i + 1, 1, b].rearrange("(d h) t -> d h t", h=H)[:, heads, :]
                            sp.dma_start(k_stack[b * 3 * HD:(b + 1) * 3 * HD, heads, :],
                                         k_rows.unsqueeze(0).broadcast_to([3, HD, HG, N]))\
                              .then_inc(stack_in[g].sem, 16)
                    elif kind == "NT":
                        g = stage[1]
                        sp.wait_ge(emptied(ph, stage), emptied_at(ph, i, stage))
                        carry(sp)
                        sp.dma_start(hbm["maxima"][i, g], mxT[:, g, :]).then_inc(mx_out[g].sem, 16)
                        sp.wait_ge(mx_out[g].sem, mx_out[g].at(i, 16))
                        carry(sp)
                        sp.dma_start(q_stack[STACK:STACK + MAXROWS, g * HG:(g + 1) * HG, :],
                                     hbm["maxima"][i, g].rearrange("(a h) t -> a h t", h=HG))\
                          .then_inc(mx_in[g].sem, 16)
                    elif kind == "YT" and n == 1:
                        sp.wait_ge(out_done.sem, out_done.at(i, 1))
                        carry(sp)
                        sp.dma_start(hbm["out"][i].rearrange("(t p) d -> p t d", p=P), out_sb[:])\
                          .then_inc(out_dma.sem, 16)

            turn(first, -1)
            with sp.Fori(0, B - 1, 1) as i:
                turn(body, i)
            turn(last, B - 1)
            if n == 1:
                sp.wait_ge(out_dma.sem, out_dma.at(B - 1, 16))

        @block.tensor
        def _(pe):
            if n == 0:
                pe.wait_ge(loaded[0], 80)
                pe.wait_ge(consts_set, 4)
                pe.wait_ge(sel_set, 1)
            def turn(ph, i):
                for stage in ph.order:
                    kind = stage[0]
                    if stage in ph.ring:
                        ps = slot[ph.slot(stage)]
                        slot_full = filled(ph, stage)
                        pe.wait_ge(emptied(ph, stage), vacant_at(ph, i, stage))
                    if kind == "XT":
                        pe.wait_ge(ln_done.sem, ln_done.next(i, 1))
                        for j in range(J):
                            last = nc.tensor.transpose(ps[:, j * P:(j + 1) * P], xn[:, j, :], ident[:])
                        last.then_inc(slot_full, 1)
                    elif kind == "QK":
                        if not ph.same(stage, ("XT",)):
                            pe.wait_ge(emptied(ph, ("XT",)), emptied_at(ph, i, ("XT",)))
                        nc.tensor.matmul(ps[:, 0:N], (wq, wk)[stage[1]], xnT_next[:], start=True, stop=True)\
                            .then_inc(slot_full, 1)
                    elif kind == "VG":
                        for j in (2 * stage[1], 2 * stage[1] + 1):
                            c0 = (j % 2) * VGW
                            last = nc.tensor.matmul(ps[:, c0:c0 + VGW], xnT_next[:, j * P:(j + 1) * P], wvg,
                                                    start=True, stop=True)
                        last.then_inc(slot_full, 1)
                    elif kind == "MS":
                        pe.wait_ge(sq_done.sem, sq_done.next(i, stage[1] + 1))
                        nc.tensor.matmul(ps[:, 0:N], head_mean[:], squares[:, stage[1], :], start=True, stop=True)\
                            .then_inc(slot_full, 1)
                    elif kind == "CW":
                        if not ph.main:
                            pe.wait_ge(sel_set, 2 - n)
                            pe.wait_ge(loaded[2], 32)
                        pe.wait_ge(cwp_done.sem, cwp_done.next(i, 1))
                        carry(pe)
                        psb = ps[:].bitcast(BF16)
                        for j in range(J):
                            last = nc.tensor.transpose(psb[0:3 * E, j * P:(j + 1) * P],
                                                       cw_parts[:, j].rearrange("p a e -> p (a e)"), ident_b[:])
                        last.then_inc(slot_full, 1)
                    elif kind == "BC":
                        e = stage[1]
                        if e == 0 and not ph.same(stage, ("CW",)):
                            pe.wait_ge(emptied(ph, ("CW",)), emptied_at(ph, i, ("CW",)))
                        nc.tensor.matmul(ps[:, 0:N], select[:, e * P:(e + 1) * P], cwT[:],
                                         start=True, stop=True).then_inc(slot_full, 1)
                    elif kind == "GG":
                        c = stage[1]
                        rows, c0 = chunk_rows(c), chunk_col(c)
                        if c == 0:
                            pe.wait_ge(hand_done.sem, hand_done.next(i, 1))
                        nc.tensor.matmul(ps[0:rows, 0:N], w_gate[:, c0:c0 + rows], xnT[:], start=True, stop=True)\
                            .then_inc(slot_full, 1)
                    elif kind == "UU":
                        c = stage[1]
                        rows, c0 = chunk_rows(c), chunk_col(c)
                        moving = xnT[:]
                        if n == 1:
                            if not ph.same(stage, ("BC", c // 3)):
                                pe.wait_ge(emptied(ph, ("BC", c // 3)), emptied_at(ph, i, ("BC", c // 3)))
                            moving = xe[:, (c // 3) % 2, :]
                        nc.tensor.matmul(ps[0:rows, 0:N], w_up[:, c0:c0 + rows], moving, start=True, stop=True)\
                            .then_inc(slot_full, 1)
                    elif kind == "DN":
                        c = stage[1]
                        rows = chunk_rows(c)
                        if c == 0:
                            pe.wait_ge(y_out.sem, y_out.at(i, 0))
                        pe.wait_ge(h_done.sem, h_done.at(i, c + 1))
                        last = nc.tensor.matmul(y_ps[:, 0:N], w_down[0:rows, c, :], hid[0:rows, c % R, :],
                                                start=(c == 0), stop=(c == C - 1 and n == 1))
                        last.then_inc(h_used.sem, 1)
                    elif kind == "M":
                        g, u = stage[1], stage[2]
                        if u == 0:
                            rows_in = stack_in[g].at if g else stack_in[g].next
                            pe.wait_ge(stack_in[g].sem, rows_in(i, 6 * 16))
                        h, j = g * HG + u // J, u % J
                        nc.tensor.matmul(ps[:, 0:N], q_stack[0:STACK, h, j * P:(j + 1) * P],
                                         k_stack[0:STACK, h, :], start=True, stop=True).then_inc(slot_full, 1)
                    elif kind == "NT":
                        g = stage[1]
                        pe.wait_ge(mxp_done.sem, mxp_done.at(i, g + 1))
                        psb = ps[:].bitcast(BF16)
                        for j in range(J):
                            last = nc.tensor.transpose(psb[0:3 * HG, j * P:(j + 1) * P],
                                                       mx_parts[:, g, j].rearrange("p a h -> p (a h)"), ident_b[:])
                        last.then_inc(slot_full, 1)
                    elif kind == "E":
                        g, j, a = stage[1:]
                        if j == 0 and a == 0:
                            pe.wait_ge(mx_in[g].sem, mx_in[g].at(i, 16))
                        h = g * HG + a
                        nc.tensor.matmul(ps[:, 0:N], k_stack[0:STACK + MAXROWS, h, j * P:(j + 1) * P],
                                         q_stack[:, h, :], start=True, stop=True).then_inc(slot_full, 1)
                    elif kind == "PV":
                        g, j = stage[1:]
                        if (g, j) == (0, 0):
                            pe.wait_ge(hand_v_done.sem, hand_v_done.at(i, 1))
                        if j == 0:
                            pe.wait_ge(pv_out.sem, pv_out.at(i, g))
                        for done in ph.last_of([("E", g, j, a) for a in range(HG)]):
                            pe.wait_ge(emptied(ph, done), emptied_at(ph, i, done))
                        for a in range(HG):
                            last = nc.tensor.matmul(pv_ps[a * VW:(a + 1) * VW, 0:N], v[:, j, g * HG + a, :],
                                                    probsT[:, j, a, :], start=(j == 0), stop=(j == J - 1),
                                                    skip_group_check=True)
                        last.then_inc(p_used.sem, 1)
                    elif kind == "AT":
                        g = stage[1]
                        pe.wait_ge(pv_out.sem, pv_out.at(i, g + 1 - 0))
                        for j in range(J):
                            last = nc.tensor.transpose(ps[:, j * P:(j + 1) * P],
                                                       pv_sb[:, g % 2, j * P:(j + 1) * P], ident[:])
                        last.then_inc(slot_full, 1)
                    elif kind == "OT":
                        if not ph.same(stage, ("AT", G - 1)):
                            pe.wait_ge(emptied(ph, ("AT", G - 1)), emptied_at(ph, i, ("AT", G - 1)))
                        for j in range(J):
                            last = nc.tensor.transpose(ps[:, j * P:(j + 1) * P], att[:, j, :], ident[:])
                        last.then_inc(slot_full, 1)
                    elif kind == "OY":
                        pe.wait_ge(emptied(ph, ("OT",)), emptied_at(ph, i, ("OT",)))
                        nc.tensor.matmul(y_ps[:, 0:N], wo, attT[:], start=False, stop=True).then_inc(y_full.sem, 1)
                    elif kind == "YT":
                        pe.wait_ge(y_out.sem, y_out.at(i, 1))
                        for j in range(J):
                            last = nc.tensor.transpose(ps[:, j * P:(j + 1) * P], y_sb[:, j * P:(j + 1) * P], ident[:])
                        last.then_inc(slot_full, 1)

            turn(first, -1)
            pe.wait_ge(loaded[3], 32 if n == 0 else 48)
            with pe.Fori(0, B - 1, 1) as i:
                turn(body, i)
            turn(last, B - 1)

        @block.scalar
        def _(sc):
            if n == 0:
                sc.wait_ge(loaded[0], 80)
            def turn(ph, i):
                for stage in ph.order:
                    kind = stage[0]
                    if stage in ph.ring:
                        ps = slot[ph.slot(stage)]
                        slot_free = emptied(ph, stage)
                    if kind == "XT":
                        sc.wait_ge(filled(ph, stage), filled_at(ph, i, stage))
                        nc.scalar.activation(xnT_next[:], ps[:, 0:N], ACT.Copy).then_inc(slot_free, 1)
                    elif kind == "QK":
                        sc.wait_ge(filled(ph, stage), filled_at(ph, i, stage))
                        a = stage[1]
                        if n == 0:
                            nc.scalar.activation(qk_raw[:, a, :], ps[:, 0:N], ACT.Identity,
                                                 bias=cols[:, a:a + 1]).then_inc(slot_free, 1)
                        else:
                            nc.scalar.activation(qk[:, a, :], ps[:, 0:N], ACT.Copy).then_inc(slot_free, 1)
                    elif kind == "MS":
                        sc.wait_ge(filled(ph, stage), filled_at(ph, i, stage))
                        nc.scalar.activation(rinv[:, stage[1], :], ps[:, 0:N], ACT.Sqrt, bias=cols[:, 5:6])\
                            .then_inc(slot_free, 1)
                    elif kind == "HI":
                        a = stage[1]
                        if n == 0:
                            sc.wait_ge(qk_done.sem, qk_done.next(i, a + 1))
                        else:
                            sc.wait_ge(emptied(ph, ("QK", a)), emptied_at(ph, i, ("QK", a)))
                        sc.wait_ge(parts_out[a].sem, parts_out[a].next(i, 0))
                        nc.scalar.activation(parts[:, a, 0], qk[:, a, :], ACT.Copy).then_inc(hi_done.sem, 1)
                    elif kind == "RT":
                        if n == 0:
                            sc.wait_ge(gate_raw.sem, gate_raw.next(i, 2))
                            nc.scalar.activation(gate[:], gate[:], ACT.Tanh, scale=0.5)\
                                .then_inc(gate_tanh.sem, 1)
                        sc.wait_ge(logits_done.sem, logits_done.next(i, 1))
                        nc.scalar.activation(probs[:, :, 0:E], logits[:], ACT.Exp).then_inc(exp_routed.sem, 1)
                    elif kind == "CW":
                        sc.wait_ge(filled(ph, stage), filled_at(ph, i, stage))
                        nc.scalar.activation(cwT[:], ps[:].bitcast(BF16)[0:3 * E, 0:N], ACT.Copy)\
                            .then_inc(slot_free, 1)
                    elif kind == "GG":
                        c = stage[1]
                        rows = chunk_rows(c)
                        sc.wait_ge(filled(ph, stage), filled_at(ph, i, stage))
                        sc.wait_ge(h_done.sem, h_done.of(i, c, c + 1 - R))
                        nc.scalar.activation(th[0:rows, c % R, :], ps[0:rows, 0:N], ACT.Tanh, scale=0.5)\
                            .then_inc(th_done.sem, 1)
                    elif kind == "UU":
                        c = stage[1]
                        rows = chunk_rows(c)
                        sc.wait_ge(filled(ph, stage), filled_at(ph, i, stage))
                        nc.scalar.activation(up[0:rows, c % R, :], ps[0:rows, 0:N], ACT.Copy, scale=0.5)\
                            .then_inc(slot_free, 1)
                    elif kind == "NT":
                        g = stage[1]
                        sc.wait_ge(filled(ph, stage), filled_at(ph, i, stage))
                        nc.scalar.activation(mxT[:, g, :], ps[:].bitcast(BF16)[0:3 * HG, 0:N], ACT.Copy)\
                            .then_inc(slot_free, 1)
                    elif kind == "E":
                        g, j, a = stage[1:]
                        sc.wait_ge(filled(ph, stage), filled_at(ph, i, stage))
                        if a == 0:
                            sc.wait_ge(p_used.sem, p_used.at(i, g * J + j + 1 - J))
                        nc.scalar.activation(probsT[:, j, a, :], ps[:, 0:N], ACT.Exp, scale=SCALE).then_inc(slot_free, 1)
                    elif kind == "PO":
                        g = stage[1]
                        sc.wait_ge(p_used.sem, p_used.at(i, (g + 1) * J))
                        nc.scalar.activation(pv_sb[:, g % 2, :], pv_ps[:], ACT.Copy).then_inc(pv_out.sem, 1)
                    elif kind == "OT":
                        sc.wait_ge(filled(ph, stage), filled_at(ph, i, stage))
                        nc.scalar.activation(attT[:], ps[:, 0:N], ACT.Copy).then_inc(slot_free, 1)
                    elif kind == "YT":
                        if n == 0:
                            sc.wait_ge(y_full.sem, y_full.at(i, 1))
                            nc.scalar.activation(y_sb[:], y_ps[:], ACT.Identity, bias=cols[:, 4:5])\
                                .then_inc(y_out.sem, 1)
                        else:
                            sc.wait_ge(h_used.sem, h_used.at(i, C))
                            nc.scalar.activation(y_sb[:], y_ps[:], ACT.Copy).then_inc(y_out.sem, 1)

            turn(first, -1)
            with sc.Fori(0, B - 1, 1) as i:
                turn(body, i)
            turn(last, B - 1)

        @block.vector
        def _(ve):
            used = [0]

            def link(ph, i, ins, alone=False):
                used[0] += 1
                ins.then_inc(dve_chain.sem, 1)
                ve.wait_ge(dve_chain.sem, ph.link(i, "dve", used[0]))
                if alone:
                    carry(ve)

            if n == 0:
                nc.vector.memset(minus_half[:], -0.5).then_inc(consts_set, 1)
                nc.vector.memset(v[:], 1.0).then_inc(consts_set, 1)
                nc.vector.memset(top2[:], NOT_THERE).then_inc(consts_set, 1)
            nc.vector.memset(probs[:], NOT_THERE).then_inc(consts_set, 1)
            if n == 0:
                ve.wait_ge(loaded[0], 80)
                nc.vector.tensor_copy(ident_b[:], ident[:]).then_inc(sel_set, 1)
                ve.wait_ge(x_in, 16)
            ve.wait_ge(consts_set, 4 if n == 0 else 1)
            def turn(ph, i):
                used[0] = 0
                for stage in ph.order:
                    kind = stage[0]
                    if stage in ph.ring:
                        ps = slot[ph.slot(stage)]
                        slot_free = emptied(ph, stage)
                    if kind == "LN":
                        for j in range(J):
                            last = nc.vector.bn_stats(stats[:, j, :], x_all[:, bass.ds(i * J + (J + j), 1), :].rearrange("p a d -> p (a d)"))
                        link(ph, i, last, alone=True)
                        for j in range(J):
                            last = nc.vector.bn_aggr(mv[:, j, :], stats[:, j, :])
                        link(ph, i, last)
                        nc.vector.tensor_scalar(var_eps[:], mv[:, :, 1], LN_EPS, None, ALU.add).then_inc(var_done.sem, 1)
                    elif kind == "XN":
                        ve.wait_ge(rstd_done.sem, rstd_done.next(i, 1))
                        for j in range(J):
                            last = nc.vector.tensor_scalar(xn[:, j, :], x_all[:, bass.ds(i * J + (J + j), 1), :].rearrange("p a d -> p (a d)"),
                                                           mv[:, j, 0:1], rstd[:, j:j + 1], ALU.subtract, ALU.mult)
                        last.then_inc(ln_done.sem, 1)
                    elif kind == "VG":
                        ve.wait_ge(filled(ph, stage), filled_at(ph, i, stage))
                        pair = slice(2 * stage[1], 2 * stage[1] + 2)
                        both = ps[:, 0:2 * VGW].rearrange("p (b w) -> p b w", b=2)
                        if n == 0:
                            bv = bias_vg[:, 0:D].unsqueeze(1).broadcast_to([P, 2, D])
                            nc.vector.tensor_tensor(v_next[:, pair, :], both[:, :, 0:D], bv, ALU.add)
                            bg = bias_vg[:, D:D + H].unsqueeze(1).broadcast_to([P, 2, H])
                            nc.vector.tensor_tensor(gate[:, pair, :], both[:, :, D:D + H], bg, ALU.add)\
                                .then_inc(gate_raw.sem, 1)
                        else:
                            nc.vector.tensor_copy(v_next[:, pair, :], both[:, :, 0:D])
                        nc.vector.tensor_copy(logits[:, pair, :], both[:, :, VGW - E:VGW]).then_inc(slot_free, 1)
                    elif kind == "RC":
                        k = stage[1]
                        if k % 2 == 0:
                            ve.wait_ge(emptied(ph, ("MS", k // 2)), emptied_at(ph, i, ("MS", k // 2)))
                        quarter = rinv[:].rearrange("p a t -> p (a t)")[:, k * 256:(k + 1) * 256]
                        nc.vector.reciprocal(quarter, quarter).then_inc(rc_done.sem, 1)
                    elif kind == "QN":
                        a = stage[1]
                        ve.wait_ge(rc_done.sem, rc_done.next(i, 2 * a + 2))
                        nc.vector.scalar_tensor_tensor(out=qk[:, a, :], in0=qk_raw[:, a, :], scalar=cols[:, 2 + a:3 + a],
                                                       in1=rinv[:, a, :], op0=ALU.mult, op1=ALU.mult)\
                            .then_inc(qk_done.sem, 1)
                    elif kind == "HAND":
                        if not ph.main:
                            ve.wait_ge(loaded[1], 32 if n == 0 else 16)
                            nc.vector.tensor_copy(select[:], select_f[:]).then_inc(sel_set, 1)
                        nc.vector.tensor_copy(xnT[:], xnT_next[:]).then_inc(hand_done.sem, 1)
                        ve.wait_ge(p_used.sem, p_used.next(i, 0))
                        for done in (("VG", 0), ("VG", 1)):
                            ve.wait_ge(emptied(ph, done), emptied_at(ph, i, done))
                        nc.vector.tensor_copy(v[:, :, :, 0:HD], v_next[:].rearrange("p j (h d) -> p j h d", h=H))\
                            .then_inc(hand_v_done.sem, 1)
                        if n == 0:
                            ve.wait_ge(gate_tanh.sem, gate_tanh.next(i, 1))
                            link(ph, i, nc.vector.tensor_scalar(gate_sig[:], gate[:], 1.0, 0.5, ALU.add, ALU.mult))
                    elif kind == "RT":
                        for done in (("VG", 0), ("VG", 1)):
                            ve.wait_ge(emptied(ph, done), emptied_at(ph, i, done))
                        link(ph, i, nc.vector.tensor_reduce(lmax[:], logits[:], AXIS.X, ALU.max))
                        nc.vector.tensor_tensor(logits[:], logits[:], lmax[:].unsqueeze(2).broadcast_to([P, J, E]),
                                                ALU.subtract).then_inc(logits_done.sem, 1)
                    elif kind == "RW":
                        p = probs[:, :, 0:E]
                        ve.wait_ge(exp_routed.sem, exp_routed.next(i, 1))
                        link(ph, i, nc.vector.tensor_reduce(psum_[:], p, AXIS.X, ALU.add))
                        link(ph, i, nc.vector.reciprocal(psum_[:], psum_[:]))
                        link(ph, i, nc.vector.tensor_tensor(p, p, psum_[:].unsqueeze(2).broadcast_to([P, J, E]), ALU.mult),
                             alone=True)
                        for j in range(J):
                            last = nc.vector.max(top8[:, j, :], probs[:, j, 0:E])
                        link(ph, i, last)
                        link(ph, i, nc.vector.tensor_copy(top2[:, :, 0:2], top8[:, :, 0:2]), alone=True)
                        for j in range(J):
                            last = nc.vector.match_replace(marked[:, j, :], top2[:, j, :], probs[:, j, :], TAKEN)
                        link(ph, i, last)
                        c_in = nc.vector.scalar_tensor_tensor(out=cw[:], in0=marked[:, :, 0:E], scalar=(NOT_THERE + TAKEN) / 2,
                                                              in1=p, op0=ALU.is_lt, op1=ALU.mult)
                        if n == 0:
                            c_in.then_inc(cw_done.sem, 1)
                        else:
                            link(ph, i, c_in)
                            link(ph, i, nc.vector.tensor_tensor(psum_[:], top8[:, :, 0], top8[:, :, 1], ALU.add))
                            link(ph, i, nc.vector.tensor_scalar(psum_[:], psum_[:], 1e-20, None, ALU.add))
                            link(ph, i, nc.vector.reciprocal(psum_[:], psum_[:]))
                            nc.vector.tensor_tensor(cw[:], cw[:], psum_[:].unsqueeze(2).broadcast_to([P, J, E]), ALU.mult)\
                                .then_inc(cw_done.sem, 1)
                    elif kind == "BC":
                        e = stage[1]
                        ve.wait_ge(filled(ph, stage), filled_at(ph, i, stage))
                        if n == 1:
                            if e == 0:
                                ve.wait_ge(hand_done.sem, hand_done.next(i, 1))
                            nc.vector.tensor_tensor(xe[:, e % 2, :], xnT[:], ps[:, 0:N], ALU.mult).then_inc(slot_free, 1)
                        else:
                            c = e + 1
                            ve.wait_ge(emptied(ph, ("UU", c)), emptied_at(ph, i, ("UU", c)))
                            ve.wait_ge(h_done.sem, h_done.of(i, c, c + 1 - R))
                            nc.vector.tensor_tensor(upc[:, c % R, :], up[:, c % R, :], ps[:, 0:N], ALU.mult)\
                                .then_inc(slot_free, 1)
                    elif kind == "GA":
                        c = stage[1]
                        rows = chunk_rows(c)
                        ps = slot[ph.slot(("GG", c))]
                        ve.wait_ge(th_done.sem, th_done.of(i, c, c + 1))
                        ve.wait_ge(h_done.sem, h_done.of(i, c, c + 1 - R))
                        ve.wait_ge(filled(ph, ("GG", c)), filled_at(ph, i, ("GG", c)))
                        nc.vector.scalar_tensor_tensor(out=act[0:rows, c % R, :], in0=th[0:rows, c % R, :], scalar=1.0,
                                                       in1=ps[0:rows, 0:N], op0=ALU.add, op1=ALU.mult)\
                            .then_inc(emptied(ph, ("GG", c)), 1)
                    elif kind == "M":
                        g, u = stage[1], stage[2]
                        ve.wait_ge(filled(ph, stage), filled_at(ph, i, stage))
                        nc.vector.tensor_reduce(mx[:, g, u // J, u % J:u % J + 1], ps[:, 0:N], AXIS.X, ALU.max)\
                            .then_inc(slot_free, 1)
                    elif kind == "AT":
                        g = stage[1]
                        ve.wait_ge(filled(ph, stage), filled_at(ph, i, stage))
                        src = ps[:, 0:N].rearrange("p (j h c) -> p j h c", j=J, h=HG)
                        link(ph, i, nc.vector.reciprocal(inv[:], src[:, :, :, HD]))
                        use = inv
                        if n == 0:
                            link(ph, i, nc.vector.tensor_tensor(inv2[:], inv[:], gate_sig[:, :, g * HG:(g + 1) * HG], ALU.mult))
                            use = inv2
                        dst = att[:, :, g * HG * HD:(g + 1) * HG * HD].rearrange("p j (h d) -> p j h d", h=HG)
                        nc.vector.tensor_tensor(dst, src[:, :, :, 0:HD], use[:].unsqueeze(3).broadcast_to([P, J, HG, HD]),
                                                ALU.mult).then_inc(slot_free, 1)
                    elif kind == "YT":
                        ve.wait_ge(filled(ph, stage), filled_at(ph, i, stage))
                        xs = x_all[:, bass.ds(i * J, J), :]
                        y = ps[:, 0:N].rearrange("p (j d) -> p j d", j=J)
                        if n == 0:
                            nc.vector.tensor_tensor(xs, xs, y, ALU.add).then_inc(slot_free, 1)
                        else:
                            ve.wait_ge(out_dma.sem, out_dma.at(i, 0))
                            nc.vector.tensor_tensor(out_sb[:], xs, y, ALU.add).then_inc(slot_free, 1)
                            ve.wait_ge(emptied(ph, stage), emptied_at(ph, i, stage))
                            nc.vector.tensor_tensor(out_sb[:], out_sb[:], att[:], ALU.add).then_inc(out_done.sem, 1)
                assert used[0] == ph.links["dve"], (n, ph.main, ph.setup, used, ph.links)

            turn(first, -1)
            with ve.Fori(0, B - 1, 1) as i:
                turn(body, i)
            turn(last, B - 1)

        @block.gpsimd
        def _(gp):
            used = [0]

            def link(ph, i, ins):
                used[0] += 1
                ins.then_inc(pool_chain.sem, 1)
                gp.wait_ge(pool_chain.sem, ph.link(i, "pool", used[0]))
                carry(gp)

            if n == 0:
                nc.gpsimd.memset(k_stack[64:96].rearrange("p h t -> p (h t)").bitcast(F32), TWO_ONES).then_inc(ones_set, 1)
            for t in (*free, *parts_out, h_done, h_used, p_used, pv_out, y_out, out_dma):
                gp.sem_inc(t.sem, t.credit)
            if n == 0:
                gp.wait_ge(consts_set, 4)
                gp.wait_ge(ones_set, 1)
            def turn(ph, i):
                used[0] = 0
                for stage in ph.order:
                    kind = stage[0]
                    if kind == "LN":
                        gp.wait_ge(var_done.sem, var_done.next(i, 1))
                        nc.gpsimd.tensor_tensor(rstd[:], var_eps[:], minus_half[:].broadcast_to([P, J]), ALU.pow)\
                            .then_inc(rstd_done.sem, 1)
                    elif kind == "SQ":
                        a = stage[1]
                        gp.wait_ge(emptied(ph, ("QK", a)), emptied_at(ph, i, ("QK", a)))
                        nc.gpsimd.tensor_tensor(squares[:, a], qk_raw[:, a], qk_raw[:, a], ALU.mult).then_inc(sq_done.sem, 1)
                    elif kind == "PT":
                        a = stage[1]
                        gp.wait_ge(hi_done.sem, hi_done.next(i, a + 1))
                        link(ph, i, nc.gpsimd.tensor_tensor(rest[:, a], qk[:, a], parts[:, a, 0], ALU.subtract))
                        link(ph, i, nc.gpsimd.tensor_tensor(parts[:, a, 1], qk[:, a], parts[:, a, 0], ALU.subtract))
                        nc.gpsimd.tensor_tensor(parts[:, a, 2], rest[:, a], parts[:, a, 1], ALU.subtract)\
                            .then_inc(parts_done.sem, 1)
                    elif kind == "RW":
                        gp.wait_ge(cw_done.sem, cw_done.next(i, 1))
                        carry(gp)
                        link(ph, i, nc.gpsimd.tensor_copy(cw_parts[:, :, 0, :], cw[:]))
                        link(ph, i, nc.gpsimd.tensor_tensor(cw_rest[:], cw[:], cw_parts[:, :, 0, :], ALU.subtract))
                        link(ph, i, nc.gpsimd.tensor_copy(cw_parts[:, :, 1, :], cw_rest[:]))
                        nc.gpsimd.tensor_tensor(cw_parts[:, :, 2, :], cw_rest[:], cw_parts[:, :, 1, :], ALU.subtract)\
                            .then_inc(cwp_done.sem, 1)
                    elif kind == "GA":
                        c = stage[1]
                        rows = chunk_rows(c)
                        if n == 1 or c == 0:
                            for done in ph.last_of([("GG", c), ("UU", c)]):
                                gp.wait_ge(emptied(ph, done), emptied_at(ph, i, done))
                            gp.wait_ge(h_used.sem, h_used.of(i, c, c + 1 - R))
                            nc.gpsimd.tensor_tensor(hid[0:rows, c % R, :], act[0:rows, c % R, :], up[0:rows, c % R, :],
                                                    ALU.mult).then_inc(h_done.sem, 1)
                    elif kind == "BC" and n == 0:
                        c = stage[1] + 1
                        for done in ph.last_of([("GG", c), stage]):
                            gp.wait_ge(emptied(ph, done), emptied_at(ph, i, done))
                        gp.wait_ge(h_used.sem, h_used.of(i, c, c + 1 - R))
                        nc.gpsimd.tensor_tensor(hid[:, c % R, :], act[:, c % R, :], upc[:, c % R, :],
                                                ALU.mult).then_inc(h_done.sem, 1)
                    elif kind == "M" and stage[2] == HG * J - 1:
                        g = stage[1]
                        for done in ph.last_of([("M", g, u) for u in range(HG * J)]):
                            gp.wait_ge(emptied(ph, done), emptied_at(ph, i, done))
                        carry(gp)
                        hi, mid, lo = (mx_parts[:, g, :, a, :] for a in range(3))
                        link(ph, i, nc.gpsimd.tensor_scalar(mx_neg[:], mx[:, g].rearrange("p h j -> p j h"), -1.0, None, ALU.mult))
                        link(ph, i, nc.gpsimd.tensor_copy(hi, mx_neg[:]))
                        link(ph, i, nc.gpsimd.tensor_tensor(mx_rest[:], mx_neg[:], hi, ALU.subtract))
                        link(ph, i, nc.gpsimd.tensor_copy(mid, mx_rest[:]))
                        nc.gpsimd.tensor_tensor(lo, mx_rest[:], mid, ALU.subtract).then_inc(mxp_done.sem, 1)
                assert used[0] == ph.links["pool"], (n, ph.main, ph.setup, used, ph.links)

            turn(first, -1)
            with gp.Fori(0, B - 1, 1) as i:
                turn(body, i)
            turn(last, B - 1)


TIMES_0 = {"up": 0.041, "gated": 0.006, "weights": 0.001, "max": 0.234, "max_span": 0.715, "max_parts": 0.22,
           "exp": 0.735, "exp_span": 0.764, "exp_lead": 2.725, "sums": 1.789, "normalise": 0.149,
           "chunks": -1.28, "span": 6.659, "lag": 0.516, "down": 0.0, "down_step": 0.2, "out": 3.873,
           "out_lag": 0.96, "result": 6.738, "norm": -3.778, "qk": 0.304, "squares": 0.678, "roots": 0.758,
           "roots_step": 0.189, "values": 4.148, "route": 0.572, "hand": 3.887, "ahead": 0.911,
           "ahead_step": 0.332, "first_values": 2.024, "first_hand": 2.649, "first_step": 1.087}
TIMES_1 = {"up": 0.001, "gated": 0.001, "weights": 0.047, "max": 0.3, "max_span": 0.762, "max_parts": 0.257,
           "exp": 0.729, "exp_span": 0.443, "exp_lead": 2.686, "sums": 1.509, "normalise": 0.139,
           "chunks": 0.262, "span": 4.113, "lag": 1.317, "down": 0.024, "down_step": 0.034, "out": 6.508,
           "out_lag": 0.747, "result": 4.793, "norm": 0.183, "qk": 0.677, "squares": 1.195, "roots": 1.412,
           "roots_step": 0.041, "values": 3.052, "route": 0.242, "hand": 3.656, "ahead": 0.174,
           "ahead_step": 1.259, "first_values": 1.988, "first_hand": 2.371, "first_step": 1.05}


def layers():
    return (
        {"n": 0, "E": 16, "chunks": 9, "hidden": 9 * P, "vgw": D + H + 16, "att_cols": 2 * D + (D + H + 16) + D,
         "times": TIMES_0, "links": {"dve": (10, 8), "pool": (11, 12)}},
        {"n": 1, "E": 8, "chunks": 24, "hidden": 8 * 352, "vgw": D + 8, "att_cols": 2 * D + (D + 8),
         "times": TIMES_1, "links": {"dve": (13, 4), "pool": (11, 12)}},
    )


def two_layers(nc, h0, h1):
    with ExitStack() as ctx:
        l0, l1 = layers()

        def sb(name, shape, dt=F32):
            return ctx.enter_context(nc.sbuf_tensor(name, shape, dt))

        shared = (sb("x_all", [P, B * J, D]), sb("ident", [P, P]), sb("ident_b", [P, P], BF16),
                  sb("k_stack", [96, H, N], BF16), sb("v", [P, J, H, VW]), sb("minus_half", [P, 1]),
                  sb("top2", [P, J, 8]), (sb("w_att_0", [P, l0["att_cols"]]), sb("w_att_1", [P, l1["att_cols"]])))
        layer_block(nc, l0, shared, h0)
        layer_block(nc, l1, shared, h1)


def kernel(**inputs):
    import numpy as np
    import concourse.bacc as bacc
    from concourse.bass_utils import run_bass_kernel_spmd

    x = {k: np.asarray(a) for k, a in inputs.items()}
    by_d = np.arange(D).reshape(H, HD).T.reshape(D)
    per_d = np.repeat(np.arange(HD), H)
    f0, f1 = x["L0_ffn_Wg"], x["L1_ffn_W1"]

    def side(a):
        return np.transpose(a, (1, 0, 2)).reshape(D, -1)

    wq0 = x["L0_attn_Wq"]
    eye = np.eye(P, dtype=np.float32)
    sel0 = np.zeros((3, 16, 8, P), np.float32)
    sel1 = np.zeros((3, 8, 8, P), np.float32)
    for c in range(8):
        sel0[:, 2 * c, c, 0:64] = 1.0
        sel0[:, 2 * c + 1, c, 64:128] = 1.0
        sel1[:, c, c, :] = 1.0
    head_mean = (np.arange(P)[:, None] % H == np.arange(P)[None] % H).astype(np.float32) / HD
    arrays0 = {
        "x": x["L0_attn_x"].reshape(B * N, D),
        "ident": eye,
        "select": sel0.reshape(48, 8 * P),
        "head_mean": head_mean,
        "cols": np.stack([x["L0_attn_bq"][:D][by_d], x["L0_attn_bk"][by_d], x["L0_attn_qn_w"][per_d],
                          x["L0_attn_kn_w"][per_d], x["L0_attn_bo"], np.full(D, RMS_EPS, np.float32)], axis=1),
        "bias_vg": np.concatenate([x["L0_attn_bv"], x["L0_attn_bq"][D:]]),
        "att": np.concatenate([wq0[:, :D][:, by_d], x["L0_attn_Wk"][:, by_d], x["L0_attn_Wv"], wq0[:, D:],
                               x["L0_ffn_Wr"], x["L0_attn_Wo"]], axis=1),
        "gate": np.concatenate([x["L0_ffn_Sg"], side(x["L0_ffn_Wg"])], axis=1),
        "up": np.concatenate([x["L0_ffn_Su"], side(x["L0_ffn_Wu"])], axis=1),
        "down": np.concatenate([x["L0_ffn_Sd"][None], x["L0_ffn_Wd"].reshape(8, P, D)]).transpose(1, 0, 2),
    }
    arrays1 = {
        "select": sel1.reshape(24, 8 * P),
        "att": np.concatenate([x["L1_attn_Wq"].T[:, by_d], x["L1_attn_Wk"].T[:, by_d], x["L1_attn_Wv"].T,
                               x["L1_ffn_Wg"].T], axis=1),
        "gate": side(np.transpose(x["L1_ffn_W1"], (0, 2, 1))),
        "up": side(np.transpose(x["L1_ffn_W3"], (0, 2, 1))),
        "down": np.transpose(x["L1_ffn_W2"], (0, 2, 1)),
    }
    nc = bacc.Bacc("TRN2", target_bir_lowering=False, num_devices=1)
    given, hbm = {}, []
    for n, arrays in enumerate((arrays0, arrays1)):
        aps = {}
        for name, a in arrays.items():
            a = np.ascontiguousarray(a)
            full = f"in{n}_{name}"
            given[full] = a
            aps[name] = nc.dram_tensor(full, a.shape, mybir.dt.from_np(a.dtype), kind="ExternalInput").ap()
        aps["parts"] = nc.dram_tensor(f"parts{n}", (B, 2, 3, P, N), BF16, kind="Internal").ap()
        aps["maxima"] = nc.dram_tensor(f"maxima{n}", (B, G, 3 * HG, N), BF16, kind="Internal").ap()
        hbm.append(aps)
    hbm[0]["next_att"] = hbm[1].pop("att")
    hbm[1]["out"] = nc.dram_tensor("out", (B, N, D), F32, kind="ExternalOutput").ap()
    two_layers(nc, hbm[0], hbm[1])
    r = run_bass_kernel_spmd(nc, [given], core_ids=[0])
    return r.results[0]["out"]
```
